# Optimizing a Trainium2 kernel written in Bass

```python
import numpy as np
import jax
import jax.numpy as jnp

def _softmax(x, axis=-1):
    return jax.nn.softmax(x, axis=axis)

def _gelu(x):
    return jax.nn.gelu(x, approximate=True)

def _silu(x):
    return jax.nn.silu(x)

def _sigmoid(x):
    return jax.nn.sigmoid(x)

def _layernorm(x, axis=-1, eps=1e-05):
    m = jnp.mean(x, axis=axis, keepdims=True)
    v = jnp.var(x, axis=axis, keepdims=True)
    return (x - m) / jnp.sqrt(v + eps)

def _scatter_add(tgt, idx, src, axis=0):
    return tgt.at[idx].add(src)

def _segment_sum(src, seg, n):
    return jax.ops.segment_sum(src, seg, n)
kernel_name = 'mk_xattn_ffn_d1_seqx_r4_9a0e3e'

def setup_inputs(seed: int=0):
    np.random.seed(seed)
    _w = jnp.asarray

    def _rec_inputs():
        import jax
        import jax.numpy as jnp
        _rk = jax.random.key(seed)
        x = -0.0002928 + 1 * jax.random.normal(jax.random.fold_in(_rk, 1), (1, 2048, 256), jnp.float32)
        _lenS = 2048 - jax.random.randint(jax.random.fold_in(_rk, 7), (1,), 0, max(1, 2048 // 4) + 1, jnp.int32)
        _lenS2 = 1601 - jax.random.randint(jax.random.fold_in(_rk, 8), (1,), 0, max(1, 1601 // 4) + 1, jnp.int32)
        _ctx_512P = jax.random.normal(jax.random.fold_in(_rk, 11), (1, 16, 128), jnp.float32)
        _ctx_512c = jax.random.dirichlet(jax.random.fold_in(_rk, 511), 0.3 * jnp.ones((16,), jnp.float32), (1, 1601))
        _ctx_512t = jnp.einsum('bsk,bkd->bsd', _ctx_512c, _ctx_512P)
        _ctx_512t = _ctx_512t * jax.lax.rsqrt(jnp.mean(jnp.square(_ctx_512t)) + 1e-12) * 0.953939
        ctx_512 = -0.000514642 + 1.00011 * (_ctx_512t + 0.3 * jax.random.normal(jax.random.fold_in(_rk, 611), (1, 1601, 128), jnp.float32))
        return (x, ctx_512)
    x, ctx_512 = _rec_inputs()

    def _L0_xattn_setup():
        import jax, jax.numpy as jnp
        import numpy as np
        DIM = 256
        LATENT_DIM = 128
        NUM_HEADS = 16
        HEAD_DIM = DIM // NUM_HEADS
        SCALE = HEAD_DIM ** (-0.5)
        key = jax.random.key(seed)
        k1, k2, k3, k4, k5 = jax.random.split(key, 5)
        B, xN, zN = (2, 512, 512)
        x = jax.random.normal(k1, (B, xN, DIM), dtype=jnp.float32)
        z = jax.random.normal(k2, (B, zN, LATENT_DIM), dtype=jnp.float32)
        Wq = jax.random.normal(k3, (DIM, DIM), dtype=jnp.float32) * DIM ** (-0.5)
        Wkv = jax.random.normal(k4, (2 * DIM, LATENT_DIM), dtype=jnp.float32) * LATENT_DIM ** (-0.5)
        Wo = jax.random.normal(k5, (DIM, DIM), dtype=jnp.float32) * DIM ** (-0.5)
        return {'x': x, 'z': z, 'Wq': Wq, 'Wkv': Wkv, 'Wo': Wo}
    _L0_xattn_all = _L0_xattn_setup()
    _L0_xattn_in = {k: v for k, v in _L0_xattn_all.items() if k in ('Wq', 'Wkv', 'Wo')}
    del _L0_xattn_all

    def _L0_ffn_setup():
        import jax, jax.numpy as jnp
        import numpy as np
        TOP_K = 2
        key = jax.random.key(seed)
        ks = jax.random.split(key, 5)
        B, T, D, E, F = (2, 512, 256, 8, 512)
        scale_d = 1.0 / np.sqrt(D)
        scale_f = 1.0 / np.sqrt(F)
        return {'x': jax.random.normal(ks[0], (B, T, D), jnp.float32), 'kernel_router_DE': jax.random.normal(ks[1], (D, E), jnp.float32) * scale_d, 'kernel_gating_EDF': jax.random.normal(ks[2], (E, D, F), jnp.float32) * scale_d, 'kernel_up_EDF': jax.random.normal(ks[3], (E, D, F), jnp.float32) * scale_d, 'kernel_down_EFD': jax.random.normal(ks[4], (E, F, D), jnp.float32) * scale_f}
    _L0_ffn_all = _L0_ffn_setup()
    _L0_ffn_in = {k: v for k, v in _L0_ffn_all.items() if k in ('kernel_router_DE', 'kernel_gating_EDF', 'kernel_up_EDF', 'kernel_down_EFD')}
    del _L0_ffn_all
    return {'x': x, 'ctx_512': ctx_512, 'L0_xattn_Wq': _L0_xattn_in['Wq'], 'L0_xattn_Wkv': _L0_xattn_in['Wkv'], 'L0_xattn_Wo': _L0_xattn_in['Wo'], 'L0_ffn_kernel_router_DE': _L0_ffn_in['kernel_router_DE'], 'L0_ffn_kernel_gating_EDF': _L0_ffn_in['kernel_gating_EDF'], 'L0_ffn_kernel_up_EDF': _L0_ffn_in['kernel_up_EDF'], 'L0_ffn_kernel_down_EFD': _L0_ffn_in['kernel_down_EFD']}

def reference(x, ctx_512, L0_xattn_Wq, L0_xattn_Wkv, L0_xattn_Wo, L0_ffn_kernel_router_DE, L0_ffn_kernel_gating_EDF, L0_ffn_kernel_up_EDF, L0_ffn_kernel_down_EFD):
    import jax
    import jax.numpy as jnp

    def _L0_xattn_ref(x, z, Wq, Wkv, Wo):
        import jax, jax.numpy as jnp
        import numpy as np
        DIM = 256
        LATENT_DIM = 128
        NUM_HEADS = 16
        HEAD_DIM = DIM // NUM_HEADS
        SCALE = HEAD_DIM ** (-0.5)
        B, xN, _ = x.shape
        _, zN, _ = z.shape
        Q = (x @ Wq.T).reshape(B, xN, NUM_HEADS, HEAD_DIM)
        KV = (z @ Wkv.T).reshape(B, zN, 2, NUM_HEADS, HEAD_DIM)
        K = KV[:, :, 0]
        V = KV[:, :, 1]
        attn = jnp.einsum('bqhd,bkhd->bhqk', Q, K) * SCALE
        attn = jax.nn.softmax(attn, axis=-1)
        O = jnp.einsum('bhqk,bkhd->bqhd', attn, V).reshape(B, xN, DIM)
        return O @ Wo.T

    def _L0_ffn_ref(x, kernel_router_DE, kernel_gating_EDF, kernel_up_EDF, kernel_down_EFD):
        import jax, jax.numpy as jnp
        import numpy as np
        TOP_K = 2
        E = kernel_router_DE.shape[-1]
        x = x.astype(jnp.float32)
        router_logits_BTE = jnp.einsum('BTD,DE->BTE', x, kernel_router_DE)
        probs_BTE = jax.nn.softmax(router_logits_BTE.astype(jnp.float32), axis=-1)
        weights_BTX, indices_BTX = jax.lax.top_k(probs_BTE, TOP_K)
        norm_weights_BTX = jax.nn.softmax(weights_BTX, axis=-1)
        one_hot_BTXE = jax.nn.one_hot(indices_BTX, num_classes=E, dtype=jnp.float32)
        full_weights_BTE = jnp.sum(one_hot_BTXE * norm_weights_BTX[..., None], axis=2)
        gating_BTEF = jnp.einsum('BTD,EDF->BTEF', x, kernel_gating_EDF)
        fuse_BTEF = jax.nn.silu(gating_BTEF) * jnp.einsum('BTD,EDF->BTEF', x, kernel_up_EDF)
        down_BTED = jnp.einsum('BTEF,EFD->BTED', fuse_BTEF, kernel_down_EFD)
        out_BTD = jnp.einsum('BTED,BTE->BTD', down_BTED, full_weights_BTE)
        return out_BTD.astype(jnp.float32)
    x = x + _L0_xattn_ref(_layernorm(x, axis=-1), ctx_512, L0_xattn_Wq, L0_xattn_Wkv, L0_xattn_Wo)
    x = x + _L0_ffn_ref(_layernorm(x, axis=-1), L0_ffn_kernel_router_DE, L0_ffn_kernel_gating_EDF, L0_ffn_kernel_up_EDF, L0_ffn_kernel_down_EFD)
    return x

_drawn_inputs = setup_inputs


def setup_inputs(seed=0):
    import zlib

    import numpy as np

    out = dict(_drawn_inputs(seed))
    spreads = {}
    factors = {}
    for name, (base, spread) in spreads.items():
        noise = np.random.default_rng([zlib.crc32(name.encode()), seed]).standard_normal(out[name].shape)
        drawn = base * np.exp(spread * noise) if base else spread * noise
        out[name] = jnp.asarray(drawn.astype(out[name].dtype))
    for name, factor in factors.items():
        out[name] = (out[name] * factor).astype(out[name].dtype)
    return out
```

```python
from contextlib import ExitStack
import struct

import concourse.bass as bass
from concourse import mybir

F32, F32R, BF16 = mybir.dt.float32, mybir.dt.float32r, mybir.dt.bfloat16
ALU = mybir.AluOpType
ACT = mybir.ActivationFunctionType
AX = mybir.AxisListType

P = 128
LN_EPS = 1e-5
CHUNK = 512
QT = CHUNK // P
QUAD = 32
HPG = P // QUAD
K_PARTS = (0, 1, 0, 2, 0, 1)
Q_PARTS = (0, 0, 1, 0, 2, 1)
BLOCKS = len(K_PARTS)
MAX_BANKS = (5, 6, 7)
O_BANK = 4
AHEAD = 20
NORM_SLOT = 30
RECIP_SLOT = 15
TURN_LAG = 3


def positive(value):
    return not isinstance(value, int) or value > 0


def slots_of(v, last):
    steady = not isinstance(v, int)
    has_next = steady or v + 1 < last
    has_after = steady or v + 2 < last
    before = steady or v > 0
    rest = [("max", 1, i) for i in range(AHEAD, 64)] if has_next else [None] * NORM_SLOT
    more = [("max", 2, i) for i in range(AHEAD)] if has_after else []
    spread = [("spread", -1, 0)] if before else []
    turn = [("turn", 1, 0)] if has_next else []
    return rest[:NORM_SLOT] + spread + rest[NORM_SLOT:] + more[:TURN_LAG] + turn + more[TURN_LAG:]


def build(nc, x, ctxT, WqT, WkvT, WoT, router, gating, up, down, out):
    T, D = x.shape
    L, KEYS = ctxT.shape
    E, _, F = gating.shape
    DT = D // P
    FT = F // P
    NTILES = T // P
    NCH = T // CHUNK
    HEADS = 16
    HD = D // HEADS
    G = HEADS // HPG
    UNITS = NCH * G
    KT = -(-KEYS // P)
    LASTK = KEYS - (KT - 1) * P
    KPAD = KEYS + KEYS % 2
    ROWS = BLOCKS * HD
    CROWS = ROWS + 3
    SCALE = float(HD) ** -0.5
    STEP = KEYS // 4
    SLOTS = 66
    MT_HEADS = P // HD
    assert L == P and HPG * (HD + 1) <= P and CROWS <= P and UNITS % 4 == 0
    PRO_SLOTS = 64 + 1 + AHEAD

    with ExitStack() as stack:
        def at(name, shape, dt, offset):
            return nc.alloc_sbuf_tensor_at(name, shape, dt, offset=offset)

        def sem(name):
            return stack.enter_context(nc.semaphore(name))

        K_BYTES = G * HPG * KPAD * 2
        Q_BYTES = UNITS * HPG * CHUNK * 2
        V_BYTES = G * KT * P * 4
        VC_BYTES = KT * P * 4
        P_BYTES = 2 * HPG * CHUNK * 4
        O_BYTES = UNITS * CHUNK * 4
        base = nc.sbuf_base + -nc.sbuf_base % 32
        end = nc.sbuf_usable_end
        k_at = base
        q_at = k_at + K_BYTES
        v_at = q_at + Q_BYTES
        vc_at = v_at + V_BYTES
        p_at = vc_at + VC_BYTES
        o_at = p_at + P_BYTES
        s_at = o_at + O_BYTES
        small = [s_at]

        def little(name, shape, dt):
            size = 4 if dt in (F32, F32R) else 2
            for n in shape[1:]:
                size *= n
            small[0] += -small[0] % 32
            t = at(name, shape, dt, small[0])
            small[0] += size
            assert small[0] <= end, name
            return t

        Kst = at("Kst", [P, G * HPG * KPAD], BF16, k_at)
        Qst = at("Qst", [P, UNITS * HPG * CHUNK], BF16, q_at)
        V = at("V", [P, G * KT * P], F32, v_at)
        Vcur = at("Vcur", [P, KT, P], F32, vc_at)
        probs = at("probs", [P, 2, HPG, CHUNK], F32, p_at)
        OT = at("OT", [P, UNITS * CHUNK], F32, o_at)
        xt = at("xt", [P, 2, QT, D], F32, p_at)
        xnT = at("xnT", [P, 2, DT, CHUNK], F32, p_at + 2 * QT * D * 4)
        ctx_sb = at("ctx_sb", [P, KEYS], F32, vc_at)
        Kp = at("Kp", [P, DT, 3, KPAD], BF16, v_at)
        Qp = at("Qp", [P, DT, 3, T], BF16, o_at)
        wq = at("wq", [P, DT, D], F32, o_at + DT * 3 * T * 2)
        wkv = at("wkv", [P, 2 * D], F32, o_at + DT * 3 * T * 2 + DT * D * 4)
        rest = at("rest", [P, 2, CHUNK], F32, o_at + DT * 3 * T * 2 + DT * D * 4 + 2 * D * 4)
        WB = (2 * DT * F + FT * D) * 4
        acc = at("acc", [P, NTILES, D], F32, q_at)
        wraw = at("wraw", [P, 3, FT * D], F32, q_at + NTILES * D * 4)
        wo = at("wo", [P, G, D], F32, q_at + NTILES * D * 4 + WB)
        wA = q_at + NTILES * D * 4 + WB + G * D * 4
        w_hi = [at("w_hi0", [P, 3, FT * D], F32R, wA), at("w_hi1", [P, 3, FT * D], F32R, k_at)]
        w_lo = [at("w_lo0", [P, 3, FT * D], F32R, wA + WB), at("w_lo1", [P, 3, FT * D], F32R, k_at + WB)]
        x2_hi = at("x2_hi", [P, DT, T], F32R, k_at + 2 * WB)
        x2_lo = at("x2_lo", [P, DT, T], F32R, v_at)
        xn2 = at("xn2", [P, 2, QT, D], F32, v_at + DT * T * 4)
        f_hi = [at("f_hi0", [P, FT, CHUNK], F32R, p_at), at("f_hi1", [P, FT, CHUNK], F32R, o_at)]
        f_lo = [at("f_lo0", [P, FT, CHUNK], F32R, p_at + FT * CHUNK * 4),
                at("f_lo1", [P, FT, CHUNK], F32R, o_at + FT * CHUNK * 4)]
        silu = at("silu", [P, 2, CHUNK], F32, o_at + 2 * FT * CHUNK * 4)
        prod = at("prod", [P, 2, CHUNK], F32, o_at + 2 * FT * CHUNK * 4 + 2 * CHUNK * 4)
        assert wA + 2 * WB <= v_at and DT * T * 4 + 2 * QT * D * 4 <= V_BYTES
        assert 2 * WB + DT * T * 4 <= K_BYTES

        ident = little("ident", [P, P], F32)
        zeros = little("zeros", [P, 1, 1], F32)
        select = little("select", [HPG, P], F32)
        mx = little("mx", [P, 64], F32)
        cmax = little("cmax", [P, 16], F32)
        negc = little("negc", [16, P], F32)
        crest = little("crest", [16, P], F32)
        cpart = little("cpart", [16, 3, P], BF16)
        osb = little("osb", [P, CHUNK], F32)
        den = little("den", [QUAD, HPG * CHUNK // QUAD], F32)
        rden = little("rden", [QUAD, HPG * CHUNK // QUAD], F32)
        rrow = little("rrow", [HPG, CHUNK], F32)
        stats = little("stats", [P, QT, 6], F32)
        mv = little("mv", [P, QT, 2], F32)
        ve = little("ve", [P, QT], F32)
        sd = little("sd", [P, QT], F32)
        rs = little("rs", [P, QT], F32)
        nt = little("nt", [P, QT], F32)
        rt = little("rt", [P, DT, E], F32)
        rt2 = little("rt2", [P, DT, 2 * E], F32R)
        iota = little("iota", [P, NTILES, E], F32)
        rbase = o_at + 2 * FT * CHUNK * 4 + 4 * CHUNK * 4
        rn = [rbase]

        def routed(name, shape):
            n = 4
            for k in shape[1:]:
                n *= k
            t = at(name, shape, F32, rn[0])
            rn[0] += n + -n % 32
            assert rn[0] <= s_at
            return t

        W8 = [P, NTILES, E]
        W1 = [P, NTILES, 1]
        logit = routed("logit", W8)
        prob = routed("prob", W8)
        hot1 = routed("hot1", W8)
        hot2 = routed("hot2", W8)
        work = routed("work", W8)
        top1 = routed("top1", W1)
        top2 = routed("top2", W1)
        pick = routed("pick", W1)
        total = routed("total", W1)
        weight = routed("weight", [P, E * NTILES])

        ps = stack.enter_context(nc.psum_tensor("ps", [P, 8, CHUNK], F32))

        s_wkv, s_wq, s_ctx = sem("s_wkv"), sem("s_wq"), sem("s_ctx")
        s_x = [sem(f"s_x{j}") for j in range(NCH)]
        s_ident, s_pfill = sem("s_ident"), sem("s_pfill")
        s_stat, s_var, s_sd, s_xn = sem("s_stat"), sem("s_var"), sem("s_sd"), sem("s_xn")
        s_chain = sem("s_chain")
        s_job = sem("s_job")
        s_high, s_rest, s_mid, s_low = sem("s_high"), sem("s_rest"), sem("s_mid"), sem("s_low")
        s_xT, s_v, s_vzero, s_vone = sem("s_xT"), sem("s_v"), sem("s_vzero"), sem("s_vone")
        s_stack = [sem(f"s_stack{g}") for g in range(G)]
        s_qmore = sem("s_qmore")
        s_score, s_prob, s_av, s_vcur = sem("s_score"), sem("s_prob"), sem("s_av"), sem("s_vcur")
        s_slot, s_free = sem("s_slot"), sem("s_free")
        s_cmax, s_csplit, s_cpart, s_crow = (sem("s_cmax"), sem("s_csplit"),
                                                     sem("s_cpart"), sem("s_crow"))
        s_osb, s_den, s_rden, s_rrow = sem("s_osb"), sem("s_den"), sem("s_rden"), sem("s_rrow")
        s_acc, s_wo, s_wozero, s_rt = sem("s_acc"), sem("s_wo"), sem("s_wozero"), sem("s_rt")
        s_proj, s_resid, s_n2, s_turn2 = sem("s_proj"), sem("s_resid"), sem("s_n2"), sem("s_turn2")
        s_h2, s_l2, s_rt2, s_logit, s_route = sem("s_h2"), sem("s_l2"), sem("s_rt2"), sem("s_logit"), sem("s_route")
        s_shift, s_exp, s_iota = sem("s_shift"), sem("s_exp"), sem("s_iota")
        s_wraw, s_whi, s_wlo = sem("s_wraw"), sem("s_whi"), sem("s_wlo")
        s_gate, s_up, s_silu, s_prod = sem("s_gate"), sem("s_up"), sem("s_silu"), sem("s_prod")
        s_fhi, s_flo, s_down, s_sum, s_out = sem("s_fhi"), sem("s_flo"), sem("s_down"), sem("s_sum"), sem("s_out")

        block = stack.enter_context(nc.Block())

        KC = [(k, min(CHUNK, KEYS - k)) for k in range(0, KEYS, CHUNK)]
        jobs = [("K", 0, kc) for kc in range(len(KC))]
        for j in range(NCH):
            jobs += [("T", j, dt) for dt in range(DT)]
            jobs += [("Q", j, mt) for mt in range(DT)]
            if j == 0:
                jobs += [("K", 1, kc) for kc in range(len(KC))]
        jobs += [("V", kt, 0) for kt in range(KT)]
        number = {job: n for n, job in enumerate(jobs)}
        splits = [job for job in jobs if job[0] in "KQ"]
        nth_split = {job: n for n, job in enumerate(splits)}
        turns = [job for job in jobs if job[0] == "T"]
        nth_turn = {job: n for n, job in enumerate(turns)}

        def part(job, p):
            kind, a, b = job
            if kind == "K":
                k0, n = KC[b]
                return Kp[:, a, p, k0:k0 + n]
            return Qp[:, b, p, a * CHUNK:(a + 1) * CHUNK]

        def width(job):
            return KC[job[2]][1] if job[0] == "K" else CHUNK

        def emptied(eng, job):
            if job[0] in "KQ":
                eng.wait_ge(s_rest, nth_split[job] + 1)
            elif job[0] == "T":
                eng.wait_ge(s_xT, nth_turn[job] + 1)
            else:
                eng.wait_ge(s_v, job[1] + 1)

        def keys_of(t):
            return P if t < KT - 1 else LASTK

        def group_of(v):
            return v % G

        def slot_base(v):
            if isinstance(v, int) and v == 0:
                return PRO_SLOTS
            if isinstance(v, int) and v == UNITS - 1:
                return PRO_SLOTS - 1 + (UNITS - 1) * SLOTS - AHEAD
            return v * SLOTS + (PRO_SLOTS - 1)

        def bank_of(v, i):
            first = PRO_SLOTS if isinstance(v, int) and v == 0 else (
                slot_base(v) if isinstance(v, int) else PRO_SLOTS - 1)
            return MAX_BANKS[(first + i) % 3]

        def normalised(eng, u):
            if isinstance(u, int) and u >= UNITS - 2:
                eng.wait_ge(s_free, slot_base(UNITS - 1) + 1 + (u - (UNITS - 2)))
            else:
                eng.wait_ge(s_free, slot_base(u + 1) + (NORM_SLOT + 1))

        def turned(u):
            if isinstance(u, int) and u == 0:
                return 64 + TURN_LAG + 1
            lag = 0 if isinstance(u, int) and u == UNITS - 1 else TURN_LAG
            return (u - 1) * SLOTS + (PRO_SLOTS - 1 + 64 - AHEAD + 1 + lag + 1)

        def each_unit(eng, body):
            body(0)
            with eng.Fori(1, UNITS - 2) as v:
                body(v)
            body(UNITS - 2)
            body(UNITS - 1)

        def piece(i):
            c, qt, q = i // 16, i // 4 % 4, i % 4
            return c, qt, q * STEP, STEP if q < 3 else KEYS - 3 * STEP

        def prologue_slots():
            ahead = [("max", 1, i) for i in range(AHEAD)]
            return [("max", 0, i) for i in range(64)] + ahead[:TURN_LAG] + [("turn", 0, 0)] + ahead[TURN_LAG:]

        def steps(eng, step):
            step(0, 1)
            with eng.Fori(0, E // 2 - 1) as i:
                for k in range(2, 10):
                    step(i, k)
            for k in range(2, 8):
                step(E // 2 - 1, k)

        TOTAL_SLOTS = slot_base(UNITS - 1) + 1
        LAST_BANK, ROUTE_BANK, TURN_BANKS = 7, O_BANK, (5, 6)

        @block.sync
        def _(sp):
            sp.dma_start(wkv[:], WkvT).then_inc(s_wkv, 16)
            sp.dma_start(ctx_sb[:], ctxT).then_inc(s_ctx, 16)
            xv = x.rearrange("(j q p) d -> j p q d", j=NCH, p=P)
            sp.dma_start(xt[:, 0], xv[0]).then_inc(s_x[0], 16)
            sp.dma_start(wq[:], WqT.rearrange("(t p) n -> p t n", p=P)).then_inc(s_wq, 16)
            sp.dma_start(xt[:, 1], xv[1]).then_inc(s_x[1], 16)
            sp.dma_start(rt[:], router.rearrange("(t p) e -> p t e", p=P)).then_inc(s_rt, 16)

            Qv = Qst[:].rearrange("p (j g c i) -> p g c j i", j=NCH, g=G, c=HPG)

            def stack_rows(mt, what):
                for h in range(mt * MT_HEADS, (mt + 1) * MT_HEADS):
                    g, c, r = h // HPG, h % HPG, (h % MT_HEADS) * HD
                    for b in range(BLOCKS):
                        rows = slice(b * HD, (b + 1) * HD)
                        if what == "K":
                            sp.dma_start(Kst[rows, h * KPAD:h * KPAD + KEYS],
                                         Kp[r:r + HD, mt, K_PARTS[b], 0:KEYS]).then_inc(s_stack[g], 16)
                        elif what == "Q0":
                            sp.dma_start(Qv[rows, g, c, 0],
                                         Qp[r:r + HD, mt, Q_PARTS[b], 0:CHUNK]).then_inc(s_stack[g], 16)
                        else:
                            sp.dma_start(Qv[rows, g, c, 1:NCH],
                                         Qp[r:r + HD, mt, Q_PARTS[b], CHUNK:T].rearrange(
                                             "p (j i) -> p j i", i=CHUNK)).then_inc(s_qmore, 16)

            sp.wait_ge(s_low, nth_split[("K", 0, len(KC) - 1)] + 1)
            stack_rows(0, "K")
            sp.wait_ge(s_low, nth_split[("Q", 0, 1)] + 1)
            stack_rows(0, "Q0")
            sp.wait_ge(s_job, number[("T", 0, DT - 1)] + 1)
            sp.dma_start(xt[:, 0], xv[2]).then_inc(s_x[2], 16)
            sp.wait_ge(s_job, number[("T", 1, DT - 1)] + 1)
            sp.dma_start(xt[:, 1], xv[3]).then_inc(s_x[3], 16)
            sp.wait_ge(s_low, nth_split[("K", 1, len(KC) - 1)] + 1)
            stack_rows(1, "Q0")
            stack_rows(1, "K")
            sp.wait_ge(s_low, len(splits))
            stack_rows(0, "Q")
            stack_rows(1, "Q")

            def send_crow(v):
                sp.wait_ge(s_cpart, v + 1)
                for p in range(3):
                    row = Qst[ROWS + p:ROWS + p + 1, bass.ds(v * (HPG * CHUNK), HPG * CHUNK)]
                    sp.dma_start(row.rearrange("o (t i) -> o t i", i=P), cpart[:, p, :]).then_inc(s_crow, 16)

            def spread_den(v):
                sp.wait_ge(s_osb, v + 1)
                sp.dma_start(den[:], osb[0:P:QUAD, :].rearrange("c (e i) -> c e i", e=QUAD // HPG)).then_inc(s_den, 16)
                sp.wait_ge(s_rden, v + 1)
                if positive(v):
                    normalised(sp, v - 1)
                sp.dma_start(rrow[:].rearrange("c (e i) -> c e i", e=QUAD // HPG), rden[:]).then_inc(s_rrow, 16)

            send_crow(0)

            def body(v):
                if positive(v):
                    spread_den(v - 1)
                if isinstance(v, int) and v == UNITS - 2:
                    sp.wait_ge(s_score, (UNITS - 2) * KT * HPG)
                    sp.dma_start(acc[:], x.rearrange("(n p) d -> p n d", p=P)).then_inc(s_acc, 16)
                    sp.wait_ge(s_wozero, 1)
                    for c in range(HPG):
                        sp.dma_start(wo[c * QUAD + 1:c * QUAD + 1 + HD, :, :],
                                     WoT.rearrange("(g c d) n -> c d g n", g=G, c=HPG)[c]).then_inc(s_wo, 16)
                    load_expert(0)
                if not isinstance(v, int) or v + 1 < UNITS:
                    send_crow(v + 1)

            def load_expert(e):
                if positive(e):
                    sp.wait_ge(s_wlo, e)
                sp.dma_start(wraw[:, 0].rearrange("p (t f) -> p t f", f=F),
                             gating.rearrange("e (t p) f -> p (e t) f", p=P)[:, bass.ds(e * DT, DT), :]).then_inc(s_wraw, 16)
                sp.dma_start(wraw[:, 1].rearrange("p (t f) -> p t f", f=F),
                             up.rearrange("e (t p) f -> p (e t) f", p=P)[:, bass.ds(e * DT, DT), :]).then_inc(s_wraw, 16)
                sp.dma_start(wraw[:, 2].rearrange("p (t n) -> p t n", n=D),
                             down.rearrange("e (t p) n -> p (e t) n", p=P)[:, bass.ds(e * FT, FT), :]).then_inc(s_wraw, 16)

            each_unit(sp, body)
            spread_den(UNITS - 1)
            with sp.Fori(1, E) as e:
                load_expert(e)
            for j in range(NCH):
                sp.wait_ge(s_sum, (E - 1) * NTILES + (j + 1) * QT)
                sp.dma_start(out.rearrange("(j q p) d -> j p q d", j=NCH, p=P)[j],
                             acc[:, j * QT:(j + 1) * QT, :]).then_inc(s_out, 16)
            sp.wait_ge(s_out, 16 * NCH)

        @block.gpsimd
        def _(pool):
            pool.memset(ident[:], 0.0).then_inc(s_pfill, 1)
            pool.wait_ge(s_pfill, 1)
            pool.affine_select(out=ident[:], in_=ident[:], compare_op=ALU.not_equal, fill=1.0, base=0,
                               pattern=[[-1, P]], channel_multiplier=1).then_inc(s_ident, 1)
            pool.memset(zeros[:], 0.0).then_inc(s_iota, 1)
            pool.memset(select[:], 1.0).then_inc(s_pfill, 1)
            pool.wait_ge(s_pfill, 2)
            pool.affine_select(out=select[:], in_=select[:], compare_op=ALU.is_ge, fill=0.0, base=0,
                               pattern=[[1, P]], channel_multiplier=-QUAD).then_inc(s_pfill, 1)
            pool.wait_ge(s_pfill, 3)
            pool.affine_select(out=select[:], in_=select[:], compare_op=ALU.is_ge, fill=0.0, base=QUAD - 1,
                               pattern=[[-1, P]], channel_multiplier=QUAD).then_inc(s_ident, 1)
            for k in range(E):
                pool.memset(iota[:, :, k:k + 1], float(k)).then_inc(s_iota, 1)
            two_ones = struct.unpack("<f", struct.pack("<I", 0x3F803F80))[0]
            pool.wait_ge(s_iota, 1 + E)
            pool.wait_ge(s_ident, 2)
            pool.memset(Kst[ROWS:CROWS, :].bitcast(F32), two_ones).then_inc(s_ident, 1)
            pool.wait_ge(s_ident, 3)

            for n, job in enumerate(splits):
                w = width(job)
                pool.wait_ge(s_mid, n + 1)
                pool.tensor_tensor(part(job, 2), rest[:, n % 2, 0:w], part(job, 1), ALU.subtract).then_inc(s_low, 1)

            for g in range(G):
                pool.wait_ge(s_stack[g], 2 * HPG * BLOCKS * 16)
            pool.memset(V[:], 0.0).then_inc(s_vzero, 1)
            pool.wait_ge(s_vzero, 1)
            pool.memset(V[:].rearrange("p (n w) -> p n w", w=QUAD)[:, :, 0:1], 1.0).then_inc(s_vone, 1)

            def copy_v(v, kt):
                n = keys_of(kt)
                if positive(v):
                    pool.wait_ge(s_av, v * KT + (kt + 1 - KT))
                pool.wait_ge(s_v, KT)
                pool.tensor_copy(Vcur[0:n, kt, :],
                                 V[0:n, bass.ds(group_of(v) * (KT * P) + kt * P, P)]).then_inc(s_vcur, 1)

            def split_c(v):
                pool.wait_ge(s_iota, 1)
                pool.wait_ge(s_free, turned(v))
                if positive(v):
                    pool.wait_ge(s_crow, v * 48)
                pool.tensor_tensor(cpart[:, 0, :], negc[:], zeros[0:16, 0].to_broadcast([16, P]), ALU.add).then_inc(s_csplit, 1)
                pool.wait_ge(s_csplit, v * 4 + 1)
                pool.tensor_tensor(crest[:], negc[:], cpart[:, 0, :], ALU.subtract).then_inc(s_csplit, 1)
                pool.wait_ge(s_csplit, v * 4 + 2)
                pool.tensor_tensor(cpart[:, 1, :], crest[:], zeros[0:16, 0].to_broadcast([16, P]), ALU.add).then_inc(s_csplit, 1)
                pool.wait_ge(s_csplit, v * 4 + 3)
                pool.tensor_tensor(negc[:], crest[:], cpart[:, 1, :], ALU.subtract).then_inc(s_csplit, 1)
                pool.wait_ge(s_csplit, v * 4 + 4)
                pool.tensor_tensor(cpart[:, 2, :], negc[:], zeros[0:16, 0].to_broadcast([16, P]), ALU.add).then_inc(s_cpart, 1)

            pool.wait_ge(s_v, KT)
            for kt in range(KT):
                copy_v(0, kt)
            split_c(0)

            def split_expert(e, half):
                pool.wait_ge(s_wraw, e * 48 + 48)
                if not isinstance(e, int):
                    pool.wait_ge(s_down, e * NTILES - NTILES)
                elif e == 1:
                    pool.wait_ge(s_score, UNITS * KT * HPG)
                pool.tensor_tensor(w_hi[half][:], wraw[:], zeros[:].to_broadcast([P, 3, FT * D]),
                                   ALU.add).then_inc(s_whi, 1)
                pool.wait_ge(s_whi, e + 1)
                pool.tensor_tensor(w_lo[half][:], wraw[:], w_hi[half][:].bitcast(F32),
                                   ALU.subtract).then_inc(s_wlo, 1)

            def body(v):
                if isinstance(v, int) and v == UNITS - 2:
                    pool.wait_ge(s_score, (UNITS - 2) * KT * HPG)
                    pool.memset(wo[:], 0.0).then_inc(s_wozero, 1)
                if isinstance(v, int) and v == UNITS - 1:
                    return
                for kt in range(KT):
                    if kt == 10:
                        split_c(v + 1)
                    copy_v(v + 1, kt)

            each_unit(pool, body)
            split_expert(0, 0)
            split_expert(1, 1)
            with pool.Fori(1, E // 2) as i:
                split_expert(i * 2, 0)
                split_expert(i * 2 + 1, 1)

        @block.scalar
        def _(act):
            def deviation(j):
                act.wait_ge(s_var, j + 1)
                act.activation(sd[:], ve[:], ACT.Sqrt).then_inc(s_sd, 1)

            def high(job):
                n = nth_split[job]
                act.wait_ge(s_job, number[job] + 1)
                act.copy(part(job, 0), ps[:, number[job] % 8, 0:width(job)]).then_inc(s_high, 1)

            def turned(job):
                _, j, dt = job
                act.wait_ge(s_job, number[job] + 1)
                if j >= 2:
                    act.wait_ge(s_job, number[("Q", j - 2, DT - 1)] + 1)
                act.copy(xnT[:, j % 2, dt, :], ps[:, number[job] % 8, :]).then_inc(s_xT, 1)

            def values(kt):
                n = keys_of(kt)
                job = number[("V", kt, 0)]
                act.wait_ge(s_job, job + 1)
                act.copy(V[0:n, :].rearrange("p (g k c w) -> p k g c w", g=G, k=KT, c=HPG)[:, kt, :, :, 1:1 + HD],
                         ps[0:n, job % 8, 0:D].rearrange("p (g c d) -> p g c d", g=G, c=HPG)).then_inc(s_v, 1)

            deviation(0)
            for job in jobs:
                if job[0] in "KQ":
                    high(job)
                elif job[0] == "T":
                    turned(job)
                else:
                    if job[1] == 0:
                        act.wait_ge(s_vone, 1)
                    values(job[1])
                if job == ("K", 0, len(KC) - 1):
                    deviation(1)
                if job == ("K", 1, len(KC) - 1):
                    deviation(2)
                if job == ("Q", 1, 1):
                    deviation(3)

            def exp(v, t, c):
                n = keys_of(t)
                act.wait_ge(s_score, v * (KT * HPG) + (t * HPG + c + 1))
                if c == 0:
                    used = v * KT + (t - 1 if t >= 2 else 0)
                    if positive(used):
                        act.wait_ge(s_av, used)
                act.activation(probs[0:n, t % 2, c, :], ps[0:n, c, :], ACT.Exp, scale=SCALE).then_inc(s_prob, 1)

            def take_output(v):
                act.wait_ge(s_av, v * KT + KT)
                if positive(v):
                    normalised(act, v - 1)
                act.copy(osb[:], ps[:, O_BANK, :]).then_inc(s_osb, 1)

            def body(v):
                for t in range(KT):
                    for c in range(HPG):
                        exp(v, t, c)
                    if t == 0 and positive(v):
                        take_output(v - 1)

            each_unit(act, body)
            take_output(UNITS - 1)

            def high2(j):
                for dt in range(DT):
                    act.wait_ge(s_turn2, j * DT + dt + 1)
                    act.copy(x2_hi[:, dt, j * CHUNK:(j + 1) * CHUNK], ps[:, TURN_BANKS[dt], :]).then_inc(s_h2, 1)

            for j in range(NCH):
                deviation(NCH + j)
                if j:
                    high2(j - 1)
            high2(NCH - 1)

            def hidden(i, k):
                n = i * 8 + k
                for f in range(FT):
                    idx = n * FT + f
                    act.wait_ge(s_gate, idx + 1)
                    if positive(idx - 1):
                        act.wait_ge(s_prod, idx - 1)
                    act.activation(silu[:, f % 2, :], ps[:, 2 * (f % 2), :], ACT.Silu).then_inc(s_silu, 1)
                    act.wait_ge(s_prod, idx + 1)
                    if positive(n - 1):
                        act.wait_ge(s_down, n * QT - QT)
                    act.copy(f_hi[k % 2][:, f, :], prod[:, f % 2, :]).then_inc(s_fhi, 1)

            hidden(0, 0)
            act.wait_ge(s_shift, 1)
            act.activation(prob[:], work[:], ACT.Exp).then_inc(s_exp, 1)
            act.wait_ge(s_shift, 2)
            act.activation(total[:], pick[:], ACT.Exp).then_inc(s_exp, 1)
            steps(act, hidden)

        @block.vector
        def _(dve):
            links = [0]

            def link(instruction):
                links[0] += 1
                instruction.then_inc(s_chain, 1)
                dve.wait_ge(s_chain, links[0])

            def norm_rows(k, src, dst):
                for q in range(QT):
                    dve.bn_stats(stats[:, q, :], src(q)).then_inc(s_stat, 1)
                dve.wait_ge(s_stat, k * 2 * QT + QT)
                for q in range(QT):
                    dve.bn_aggr(mv[:, q, :], stats[:, q, :]).then_inc(s_stat, 1)
                dve.wait_ge(s_stat, (k + 1) * 2 * QT)
                dve.tensor_scalar(ve[:], mv[:, :, 1], LN_EPS, None, ALU.add).then_inc(s_var, 1)
                dve.wait_ge(s_sd, k + 1)
                link(dve.reciprocal(rs[:], sd[:]))
                link(dve.tensor_tensor(nt[:], rs[:], rs[:], ALU.mult))
                link(dve.tensor_tensor(nt[:], nt[:], ve[:], ALU.mult))
                link(dve.tensor_scalar(nt[:], nt[:], -0.5, 1.5, ALU.mult, ALU.add))
                link(dve.tensor_tensor(rs[:], rs[:], nt[:], ALU.mult))
                for q in range(QT):
                    last = dve.tensor_scalar(dst(q), src(q), mv[:, q, 0:1], rs[:, q:q + 1],
                                             ALU.subtract, ALU.mult)
                    if q < QT - 1:
                        last.then_inc(s_chain, 1)
                        links[0] += 1
                return last

            def norm1(j):
                dve.wait_ge(s_x[j], 16)
                norm_rows(j, lambda q: xt[:, j % 2, q, :], lambda q: xt[:, j % 2, q, :]).then_inc(s_xn, 1)

            def split(job):
                n, w = nth_split[job], width(job)
                dve.wait_ge(s_high, n + 1)
                if n >= 2:
                    dve.wait_ge(s_low, n - 1)
                dve.tensor_tensor(rest[:, n % 2, 0:w], ps[:, number[job] % 8, 0:w], part(job, 0),
                                  ALU.subtract).then_inc(s_rest, 1)
                dve.wait_ge(s_rest, n + 1)
                dve.tensor_copy(part(job, 1), rest[:, n % 2, 0:w]).then_inc(s_mid, 1)

            norm1(0)
            dve.wait_ge(s_rt, 16)
            link(dve.tensor_copy(rt2[:, :, 0:E], rt[:]))
            dve.tensor_tensor(rt2[:, :, E:2 * E], rt[:], rt2[:, :, 0:E].bitcast(F32), ALU.subtract).then_inc(s_rt2, 1)
            for job in jobs:
                if job[0] in "KQ":
                    split(job)
                if job == ("K", 0, len(KC) - 1):
                    norm1(1)
                if job == ("K", 1, len(KC) - 1):
                    norm1(2)
                if job == ("Q", 1, 1):
                    norm1(3)

            def slot(v, count, bank, what, u):
                kind, _, i = what
                dve.wait_ge(s_slot, count)
                if kind == "max":
                    n = piece(i)[3]
                    dve.tensor_reduce(mx[:, i:i + 1], ps[:, bank, 0:n], AX.X, ALU.max).then_inc(s_free, 1)
                elif kind == "turn":
                    if positive(u):
                        dve.wait_ge(s_cpart, u)
                    dve.tensor_scalar(negc[:], ps[0:16, bank, 0:P], -1.0, None, ALU.mult).then_inc(s_free, 1)
                else:
                    dve.tensor_tensor(OT[:, bass.ds(u * CHUNK, CHUNK)], osb[:], ps[:, bank, :],
                                      ALU.mult).then_inc(s_free, 1)

            def row_max(u, count):
                dve.wait_ge(s_free, count)
                dve.tensor_reduce(cmax[:], mx[:].rearrange("p (a b) -> p a b", b=4), AX.X,
                                  ALU.max).then_inc(s_cmax, 1)
                dve.wait_ge(s_cmax, u + 1)

            def invert(u):
                dve.wait_ge(s_den, u * 16 + 16)
                if positive(u):
                    dve.wait_ge(s_rrow, u * 16)
                dve.reciprocal(rden[:], den[:]).then_inc(s_rden, 1)

            pro = prologue_slots()
            for i, what in enumerate(pro):
                slot(0, i + 1, MAX_BANKS[i % 3], what, what[1])
                if what == ("max", 0, 63):
                    row_max(0, i + 1)

            def body(v):
                first = slot_base(v)
                n = 0
                for i, what in enumerate(slots_of(v, UNITS)):
                    if i == RECIP_SLOT and positive(v):
                        invert(v - 1)
                    if what is None:
                        continue
                    slot(v, first + (n + 1), bank_of(v, n), what, v + what[1])
                    n += 1
                    if what == ("max", 1, 63):
                        row_max(v + 1, first + n)

            each_unit(dve, body)

            def residual(j):
                for q in range(QT):
                    n = j * QT + q
                    dve.wait_ge(s_proj, n + 1)
                    dve.tensor_tensor(acc[:, n, :], ps[:, n % 4, 0:D], acc[:, n, :], ALU.add).then_inc(s_resid, 1)
                dve.wait_ge(s_resid, (j + 1) * QT)
                if j >= 2:
                    dve.wait_ge(s_turn2, (j - 1) * DT)
                norm_rows(NCH + j, lambda q: acc[:, j * QT + q, :], lambda q: xn2[:, j % 2, q, :]).then_inc(s_n2, 1)

            def low2(j):
                for dt in range(DT):
                    cols = slice(j * CHUNK, (j + 1) * CHUNK)
                    dve.wait_ge(s_h2, j * DT + dt + 1)
                    dve.tensor_tensor(x2_lo[:, dt, cols], ps[:, TURN_BANKS[dt], :],
                                      x2_hi[:, dt, cols].bitcast(F32), ALU.subtract).then_inc(s_l2, 1)

            dve.wait_ge(s_acc, 16)
            residual(0)
            invert(UNITS - 1)
            residual(1)
            low2(0)
            dve.wait_ge(s_slot, TOTAL_SLOTS + 1)
            dve.tensor_tensor(OT[:, (UNITS - 1) * CHUNK:UNITS * CHUNK], osb[:], ps[:, LAST_BANK, :],
                              ALU.mult).then_inc(s_free, 1)
            residual(2)
            low2(1)
            residual(3)
            low2(2)
            low2(3)

            def product(i, k):
                n = i * 8 + k
                for f in range(FT):
                    idx = n * FT + f
                    dve.wait_ge(s_up, idx + 1)
                    dve.wait_ge(s_silu, idx + 1)
                    if positive(idx - 1):
                        dve.wait_ge(s_fhi, idx - 1)
                    dve.tensor_tensor(prod[:, f % 2, :], silu[:, f % 2, :], ps[:, 2 * (f % 2) + 1, :],
                                      ALU.mult).then_inc(s_prod, 1)
                    dve.wait_ge(s_fhi, idx + 1)
                    dve.tensor_tensor(f_lo[k % 2][:, f, :], prod[:, f % 2, :], f_hi[k % 2][:, f, :].bitcast(F32),
                                      ALU.subtract).then_inc(s_flo, 1)

            def add_up(i, k):
                n = i * 8 + k
                e = i * 2 + k // 4
                for q in range(QT):
                    tile = k % 4 * QT + q
                    dve.wait_ge(s_down, n * QT + (q + 1))
                    dve.scalar_tensor_tensor(acc[:, tile, :], ps[:, 4 + q, 0:D],
                                             weight[:, bass.ds(e * NTILES + tile, 1)], acc[:, tile, :],
                                             op0=ALU.mult, op1=ALU.add).then_inc(s_sum, 1)

            def step(i, k):
                product(i, k)
                add_up(i, k - 1)

            def route():
                wide = lambda a: a[:].to_broadcast(W8)
                lv = ps[:, ROUTE_BANK, 0:NTILES * 2 * E].rearrange("p (n w) -> p n w", w=2 * E)
                dve.wait_ge(s_logit, 1)
                link(dve.tensor_copy(logit[:], lv[:, :, 0:E]))
                link(dve.tensor_tensor(logit[:], logit[:], lv[:, :, E:2 * E], ALU.add))
                link(dve.tensor_reduce(top1[:], logit[:], AX.X, ALU.max))
                dve.tensor_tensor(work[:], logit[:], wide(top1), ALU.subtract).then_inc(s_shift, 1)
                dve.wait_ge(s_exp, 1)
                link(dve.tensor_reduce(total[:], prob[:], AX.X, ALU.add))
                link(dve.reciprocal(pick[:], total[:]))
                link(dve.tensor_tensor(prob[:], prob[:], wide(pick), ALU.mult))

                def first_largest(top, hot):
                    link(dve.tensor_reduce(top[:], prob[:], AX.X, ALU.max))
                    link(dve.tensor_tensor(hot[:], prob[:], wide(top), ALU.is_equal))
                    link(dve.scalar_tensor_tensor(work[:], hot[:], -float(E), iota[:], op0=ALU.mult, op1=ALU.add))
                    link(dve.tensor_reduce(pick[:], work[:], AX.X, ALU.min))
                    link(dve.tensor_tensor(hot[:], work[:], wide(pick), ALU.is_equal))

                dve.wait_ge(s_iota, 1 + E)
                first_largest(top1, hot1)
                link(dve.scalar_tensor_tensor(prob[:], hot1[:], -2.0, prob[:], op0=ALU.mult, op1=ALU.add))
                first_largest(top2, hot2)
                dve.tensor_tensor(pick[:], top2[:], top1[:], ALU.subtract).then_inc(s_shift, 1)
                dve.wait_ge(s_exp, 2)
                link(dve.tensor_scalar(top1[:], total[:], 1.0, None, ALU.add))
                link(dve.reciprocal(top1[:], top1[:]))
                link(dve.tensor_tensor(top2[:], total[:], top1[:], ALU.mult))
                link(dve.tensor_tensor(hot1[:], hot1[:], wide(top1), ALU.mult))
                link(dve.tensor_tensor(hot2[:], hot2[:], wide(top2), ALU.mult))
                dve.tensor_tensor(weight[:].rearrange("p (e n) -> p n e", n=NTILES), hot1[:], hot2[:],
                                  ALU.add).then_inc(s_route, 1)
                dve.wait_ge(s_route, 1)

            product(0, 0)
            route()
            steps(dve, step)
            add_up(E // 2 - 1, 7)

        @block.tensor
        def _(pe):
            pe.wait_ge(s_wkv, 16)
            pe.wait_ge(s_ctx, 16)
            for n, job in enumerate(jobs):
                kind, a, b = job
                bank = ps[:, n % 8, :]
                if n >= 8:
                    emptied(pe, jobs[n - 8])
                if kind == "K":
                    k0, w = KC[b]
                    pe.matmul(bank[:, 0:w], wkv[:, a * P:(a + 1) * P], ctx_sb[:, k0:k0 + w],
                              start=True, stop=True).then_inc(s_job, 1)
                elif kind == "T":
                    pe.wait_ge(s_ident, 1)
                    pe.wait_ge(s_xn, a + 1)
                    for q in range(QT):
                        mm = pe.transpose(bank[:, q * P:(q + 1) * P], xt[:, a % 2, q, b * P:(b + 1) * P], ident[:])
                    mm.then_inc(s_job, 1)
                elif kind == "Q":
                    pe.wait_ge(s_wq, 16)
                    pe.wait_ge(s_xT, (a + 1) * DT)
                    for dt in range(DT):
                        mm = pe.matmul(bank, wq[:, dt, b * P:(b + 1) * P], xnT[:, a % 2, dt, :],
                                       start=(dt == 0), stop=(dt == DT - 1))
                    mm.then_inc(s_job, 1)
                else:
                    w = keys_of(a)
                    pe.matmul(bank[0:w, 0:D], ctx_sb[:, a * P:a * P + w], wkv[:, D:2 * D],
                              start=True, stop=True).then_inc(s_job, 1)
            for job in jobs[-8:]:
                emptied(pe, job)

            def slot(v, before, bank, what, u, gate=True):
                kind, _, i = what
                if positive(before - 2):
                    pe.wait_ge(s_free, before - 2)
                if kind == "max":
                    c, qt, k0, n = piece(i)
                    g = group_of(u)
                    pe.matmul(ps[:, bank, 0:n],
                              Qst[0:ROWS, bass.ds(u * (HPG * CHUNK) + (c * CHUNK + qt * P), P)],
                              Kst[0:ROWS, bass.ds(g * (HPG * KPAD) + (c * KPAD + k0), n)],
                              start=True, stop=True).then_inc(s_slot, 1)
                elif kind == "turn":
                    pe.wait_ge(s_cmax, u + 1)
                    pe.transpose(ps[0:16, bank, 0:P], cmax[:], ident[:]).then_inc(s_slot, 1)
                else:
                    pe.wait_ge(s_rrow, u * 16 + 16)
                    pe.matmul(ps[:, bank, :], select[:], rrow[:], start=True, stop=True).then_inc(s_slot, 1)

            def stacked(g):
                pe.wait_ge(s_stack[g], 2 * HPG * BLOCKS * 16)

            pe.wait_ge(s_ident, 3)
            stacked(0)
            for i, what in enumerate(prologue_slots()):
                if what == ("max", 1, 0):
                    stacked(1)
                slot(0, i, MAX_BANKS[i % 3], what, what[1])

            def score(v, t, c):
                n = keys_of(t)
                g = group_of(v)
                done = v * (KT * HPG) + (t * HPG + c + 1 - HPG)
                if positive(done):
                    pe.wait_ge(s_prob, done)
                pe.matmul(ps[0:n, c, :],
                          Kst[0:CROWS, bass.ds(g * (HPG * KPAD) + (c * KPAD + t * P), n)],
                          Qst[0:CROWS, bass.ds(v * (HPG * CHUNK) + c * CHUNK, CHUNK)],
                          start=True, stop=True).then_inc(s_score, 1)

            def attend(v, t):
                n = keys_of(t)
                pe.wait_ge(s_prob, v * (KT * HPG) + (t * HPG + HPG))
                pe.wait_ge(s_vcur, v * KT + (t + 1))
                if t == 0 and positive(v):
                    pe.wait_ge(s_osb, v)
                for c in range(HPG):
                    mm = pe.matmul(ps[c * QUAD:(c + 1) * QUAD, O_BANK, :], Vcur[0:n, t, c * QUAD:(c + 1) * QUAD],
                                   probs[0:n, t % 2, c, :], start=(t == 0), stop=(t == KT - 1))
                mm.then_inc(s_av, 1)

            def body(v):
                first = slot_base(v)
                todo = list(enumerate(slots_of(v, UNITS)))
                n = [0]

                def next_slot():
                    if not todo:
                        return
                    _, what = todo.pop(0)
                    if what is None:
                        return
                    if isinstance(v, int) and v == 0 and what == ("max", 2, 0):
                        stacked(2)
                    slot(v, first + n[0], bank_of(v, n[0]), what, v + what[1])
                    n[0] += 1

                pe.wait_ge(s_crow, v * 48 + 48)
                for t in range(KT):
                    for c in range(HPG):
                        score(v, t, c)
                        next_slot()
                    if t:
                        attend(v, t - 1)
                    elif positive(v):
                        attend(v - 1, KT - 1)
                    next_slot()
                while todo:
                    next_slot()
                if isinstance(v, int) and v == 0:
                    stacked(3)
                    pe.wait_ge(s_qmore, HEADS * BLOCKS * 16)

            each_unit(pe, body)
            attend(UNITS - 1, KT - 1)

            def project(j):
                normalised(pe, (j + 1) * G - 1)
                for q in range(QT):
                    n = j * QT + q
                    if n >= 4:
                        pe.wait_ge(s_resid, n - 3)
                    for g in range(G):
                        mm = pe.matmul(ps[:, n % 4, 0:D], OT[:, (j * G + g) * CHUNK + q * P:(j * G + g) * CHUNK + (q + 1) * P],
                                       wo[:, g, :], start=(g == 0), stop=(g == G - 1))
                    mm.then_inc(s_proj, 1)

            def turn2(j):
                pe.wait_ge(s_n2, j + 1)
                if j:
                    pe.wait_ge(s_l2, j * DT)
                for dt in range(DT):
                    for q in range(QT):
                        mm = pe.transpose(ps[:, TURN_BANKS[dt], q * P:(q + 1) * P],
                                          xn2[:, j % 2, q, dt * P:(dt + 1) * P], ident[:])
                    mm.then_inc(s_turn2, 1)

            pe.wait_ge(s_wo, HPG * 16)
            pe.wait_ge(s_free, TOTAL_SLOTS)
            project(0)
            project(1)
            turn2(0)
            pe.wait_ge(s_rrow, UNITS * 16)
            pe.matmul(ps[:, LAST_BANK, :], select[:], rrow[:], start=True, stop=True).then_inc(s_slot, 1)
            project(2)
            turn2(1)
            project(3)
            turn2(2)
            turn2(3)

            def gate_up(i, k):
                n = i * 8 + k
                j, half = k % 4, k // 4 % 2
                cols = slice(j * CHUNK, (j + 1) * CHUNK)
                pe.wait_ge(s_l2, (j + 1) * DT)
                if j == 0:
                    pe.wait_ge(s_wlo, i * 2 + (k // 4 + 1))
                for f in range(FT):
                    idx = n * FT + f
                    for m, (filled, used) in enumerate(((s_gate, s_silu), (s_up, s_prod))):
                        if positive(idx - 1):
                            pe.wait_ge(used, idx - 1)
                        pairs = [(w, r, dt) for dt in range(DT) for w, r in
                                 ((w_hi, x2_hi), (w_hi, x2_lo), (w_lo, x2_hi))]
                        for a, (w, r, dt) in enumerate(pairs):
                            mm = pe.matmul(ps[:, 2 * (f % 2) + m, :],
                                           w[half][:, m, dt * F + f * P:dt * F + (f + 1) * P], r[:, dt, cols],
                                           start=(a == 0), stop=(a == len(pairs) - 1))
                        mm.then_inc(filled, 1)

            def down_rows(i, k):
                n = i * 8 + k
                half = k // 4 % 2
                pe.wait_ge(s_flo, n * FT + FT)
                for q in range(QT):
                    if positive(n):
                        pe.wait_ge(s_sum, n * QT + (q + 1 - QT))
                    pairs = [(a, w, f) for f in range(FT) for a, w in
                             ((f_hi, w_hi), (f_hi, w_lo), (f_lo, w_hi))]
                    for b, (a, w, f) in enumerate(pairs):
                        mm = pe.matmul(ps[:, 4 + q, 0:D], a[k % 2][:, f, q * P:(q + 1) * P],
                                       w[half][:, 2, f * D:(f + 1) * D], start=(b == 0), stop=(b == len(pairs) - 1))
                    mm.then_inc(s_down, 1)

            pe.wait_ge(s_resid, NTILES)
            gate_up(0, 0)
            pe.wait_ge(s_rt2, 1)
            pe.wait_ge(s_l2, NCH * DT)
            for n in range(NTILES):
                pairs = [(r, dt) for r in (x2_hi, x2_lo) for dt in range(DT)]
                for a, (r, dt) in enumerate(pairs):
                    mm = pe.matmul(ps[:, ROUTE_BANK, n * 2 * E:(n + 1) * 2 * E], r[:, dt, n * P:(n + 1) * P],
                                   rt2[:, dt, :], start=(a == 0), stop=(a == len(pairs) - 1))
            mm.then_inc(s_logit, 1)

            def step(i, k):
                gate_up(i, k)
                if isinstance(i, int) and i == 0 and k == 1:
                    pe.wait_ge(s_route, 1)
                down_rows(i, k - 1)

            steps(pe, step)
            down_rows(E // 2 - 1, 7)


def kernel(x, ctx_512, L0_xattn_Wq, L0_xattn_Wkv, L0_xattn_Wo, L0_ffn_kernel_router_DE,
           L0_ffn_kernel_gating_EDF, L0_ffn_kernel_up_EDF, L0_ffn_kernel_down_EFD):
    import numpy as np
    import concourse.bacc as bacc
    from concourse.bass_utils import run_bass_kernel_spmd

    laid = {
        "x": np.asarray(x)[0],
        "ctxT": np.asarray(ctx_512)[0].T,
        "WqT": np.asarray(L0_xattn_Wq).T,
        "WkvT": np.asarray(L0_xattn_Wkv).T,
        "WoT": np.asarray(L0_xattn_Wo).T,
        "router": L0_ffn_kernel_router_DE,
        "gating": L0_ffn_kernel_gating_EDF,
        "up": L0_ffn_kernel_up_EDF,
        "down": L0_ffn_kernel_down_EFD,
    }
    nc = bacc.Bacc("TRN2", target_bir_lowering=False, num_devices=1)
    arrays, args = {}, {}
    for name, a in laid.items():
        a = np.ascontiguousarray(a)
        arrays[f"in_{name}"] = a
        args[name] = nc.dram_tensor(f"in_{name}", a.shape, mybir.dt.from_np(a.dtype), kind="ExternalInput").ap()
    shape = laid["x"].shape
    args["out"] = nc.dram_tensor("out_x", shape, F32, kind="ExternalOutput").ap()
    build(nc, **args)
    r = run_bass_kernel_spmd(nc, [arrays], core_ids=[0])
    return r.results[0]["out_x"].reshape((1,) + shape)
```

```python
from contextlib import ExitStack
import struct

import concourse.bass as bass
from concourse import mybir

F32, F32R, BF16 = mybir.dt.float32, mybir.dt.float32r, mybir.dt.bfloat16
ALU = mybir.AluOpType
ACT = mybir.ActivationFunctionType
AX = mybir.AxisListType

P = 128
LN_EPS = 1e-5
CHUNK = 512
QT = CHUNK // P
QUAD = 32
HPG = P // QUAD
K_PARTS = (0, 1, 0, 2, 0, 1)
Q_PARTS = (0, 0, 1, 0, 2, 1)
BLOCKS = len(K_PARTS)
MAX_BANKS = (5, 6, 7)
JOB_BANKS = 5
O_BANK = 4
AHEAD = 24
NORM_SLOT = 30
SPLIT_AT = 7
RECIP_SLOT = 15
TURN_LAG = 5


def positive(value):
    return not isinstance(value, int) or value > 0


def slots_of(v, last):
    steady = not isinstance(v, int)
    has_next = steady or v + 1 < last
    has_after = steady or v + 2 < last
    before = steady or v > 0
    rest = [("max", 1, i) for i in range(AHEAD, 64)] if has_next else [None] * NORM_SLOT
    more = [("max", 2, i) for i in range(AHEAD)] if has_after else []
    spread = [("spread", -1, 0)] if before else []
    turn = [("turn", 1, 0)] if has_next else []
    return rest[:NORM_SLOT] + spread + rest[NORM_SLOT:] + more[:TURN_LAG] + turn + more[TURN_LAG:]


def build(nc, x, ctxT, WqT, WkvT, WoT, router, gating, up, down, out):
    T, D = x.shape
    L, KEYS = ctxT.shape
    E, _, F = gating.shape
    DT = D // P
    FT = F // P
    NTILES = T // P
    NCH = T // CHUNK
    HEADS = 16
    HD = D // HEADS
    G = HEADS // HPG
    UNITS = NCH * G
    KT = -(-KEYS // P)
    LASTK = KEYS - (KT - 1) * P
    KPAD = KEYS + KEYS % 2
    ROWS = BLOCKS * HD
    CROWS = ROWS + 3
    SCALE = float(HD) ** -0.5
    STEP = KEYS // 4
    SLOTS = 66
    MT_HEADS = P // HD
    assert KT % 2 == 1 and L == P and HPG * (HD + 1) <= P and CROWS <= P and UNITS % 4 == 0
    PRO_SLOTS = 64 + 1 + AHEAD

    with ExitStack() as stack:
        def at(name, shape, dt, offset):
            return nc.alloc_sbuf_tensor_at(name, shape, dt, offset=offset)

        def sem(name):
            return stack.enter_context(nc.semaphore(name))

        K_BYTES = G * HPG * KPAD * 2
        Q_BYTES = UNITS * HPG * CHUNK * 2
        V_BYTES = G * KT * P * 4
        VC_BYTES = KT * P * 4
        P_BYTES = 2 * HPG * CHUNK * 4
        O_BYTES = UNITS * CHUNK * 4
        base = nc.sbuf_base + -nc.sbuf_base % 32
        end = nc.sbuf_usable_end
        k_at = base
        q_at = k_at + K_BYTES
        v_at = q_at + Q_BYTES
        vc_at = v_at + V_BYTES
        p_at = vc_at + VC_BYTES
        o_at = p_at + P_BYTES
        s_at = o_at + O_BYTES
        small = [s_at]

        def little(name, shape, dt):
            size = 4 if dt in (F32, F32R) else 2
            for n in shape[1:]:
                size *= n
            small[0] += -small[0] % 32
            t = at(name, shape, dt, small[0])
            small[0] += size
            assert small[0] <= end, name
            return t

        Kst = at("Kst", [P, G * HPG * KPAD], BF16, k_at)
        Qst = at("Qst", [P, UNITS * HPG * CHUNK], BF16, q_at)
        V = at("V", [P, G * KT * P], F32, v_at)
        Vcur = at("Vcur", [P, KT, P], F32, vc_at)
        probs = at("probs", [P, 2, HPG, CHUNK], F32, p_at)
        OT = at("OT", [P, UNITS * CHUNK], F32, o_at)
        xt = at("xt", [P, NCH, QT, D], F32, p_at)
        ctx_sb = at("ctx_sb", [P, KEYS], F32, vc_at)
        Kp = at("Kp", [P, DT, 3, KPAD], BF16, v_at)
        Qp = at("Qp", [P, DT, 3, T], BF16, o_at)
        wq = at("wq", [P, DT, D], F32, o_at + DT * 3 * T * 2)
        wkv = at("wkv", [P, 2 * D], F32, o_at + DT * 3 * T * 2 + DT * D * 4)
        xnT = [at("xnT0", [P, DT, CHUNK], F32, o_at + DT * 3 * T * 2 + DT * D * 4 + 2 * D * 4),
               at("xnT1", [P, DT, CHUNK], F32, v_at + DT * 3 * KPAD * 2 + 8)]
        WB = (2 * DT * F + FT * D) * 4
        acc = at("acc", [P, NTILES, D], F32, q_at)
        wraw = at("wraw", [P, 3, FT * D], F32, q_at + NTILES * D * 4)
        wo = at("wo", [P, G, D], F32, q_at + NTILES * D * 4 + WB)
        wA = q_at + NTILES * D * 4 + WB + G * D * 4
        w_hi = [at("w_hi0", [P, 3, FT * D], F32R, wA), at("w_hi1", [P, 3, FT * D], F32R, k_at)]
        w_lo = [at("w_lo0", [P, 3, FT * D], F32R, wA + WB), at("w_lo1", [P, 3, FT * D], F32R, k_at + WB)]
        x2_hi = at("x2_hi", [P, DT, T], F32R, k_at + 2 * WB)
        x2_lo = at("x2_lo", [P, DT, T], F32R, v_at)
        xn2 = at("xn2", [P, 2, QT, D], F32, v_at + DT * T * 4)
        lrows = at("lrows", [2 * E, NCH, CHUNK], F32, v_at + DT * T * 4 + 2 * QT * D * 4)
        f_hi = [at("f_hi0", [P, FT, CHUNK], F32R, p_at), at("f_hi1", [P, FT, CHUNK], F32R, o_at)]
        f_lo = [at("f_lo0", [P, FT, CHUNK], F32R, p_at + FT * CHUNK * 4),
                at("f_lo1", [P, FT, CHUNK], F32R, o_at + FT * CHUNK * 4)]
        silu = at("silu", [P, 2, CHUNK], F32, o_at + 2 * FT * CHUNK * 4)
        prod = at("prod", [P, 2, CHUNK], F32, o_at + 2 * FT * CHUNK * 4 + 2 * CHUNK * 4)
        assert wA + 2 * WB <= v_at and DT * T * 4 + 2 * QT * D * 4 <= V_BYTES
        assert 2 * WB + DT * T * 4 <= K_BYTES
        assert DT * T * 4 + 2 * QT * D * 4 + NCH * CHUNK * 4 <= V_BYTES + VC_BYTES

        ident = little("ident", [P, P], F32)
        zeros = little("zeros", [P, 1, 1], F32)
        select = little("select", [HPG, P], F32)
        mx = little("mx", [P, 64], F32)
        cmax = little("cmax", [P, 16], F32)
        negc = little("negc", [16, P], F32)
        crest = little("crest", [16, P], F32)
        cpart = little("cpart", [16, 3, P], BF16)
        osb = little("osb", [P, CHUNK], F32)
        rest = [at("rest0", [P, CHUNK], F32, small[0] - CHUNK * 4), little("rest1", [P, CHUNK], F32)]
        rrow = at("rrow", [HPG, CHUNK], F32, small[0] - CHUNK * 4)
        den = little("den", [QUAD, HPG * CHUNK // QUAD], F32)
        rden = little("rden", [QUAD, HPG * CHUNK // QUAD], F32)
        stats = little("stats", [P, QT, 6], F32)
        mv = little("mv", [P, QT, 2], F32)
        ve = little("ve", [P, QT], F32)
        sd = little("sd", [P, QT], F32)
        rs = little("rs", [P, QT], F32)
        nt = little("nt", [P, QT], F32)
        rt = little("rt", [P, DT, E], F32)
        rt2 = little("rt2", [P, DT, 2 * E], F32R)
        iota = little("iota", [P, NTILES, E], F32)
        rbase = o_at + 2 * FT * CHUNK * 4 + 4 * CHUNK * 4
        rn = [rbase]

        def routed(name, shape):
            n = 4
            for k in shape[1:]:
                n *= k
            t = at(name, shape, F32, rn[0])
            rn[0] += n + -n % 32
            assert rn[0] <= s_at
            return t

        W8 = [P, NTILES, E]
        W1 = [P, NTILES, 1]
        logit = routed("logit", W8)
        prob = routed("prob", W8)
        hot1 = routed("hot1", W8)
        hot2 = routed("hot2", W8)
        work = routed("work", W8)
        top1 = routed("top1", W1)
        top2 = routed("top2", W1)
        pick = routed("pick", W1)
        total = routed("total", W1)
        weight = routed("weight", [P, E * NTILES])

        ps = stack.enter_context(nc.psum_tensor("ps", [P, 8, CHUNK], F32))

        s_wkv, s_wq, s_ctx = sem("s_wkv"), sem("s_wq"), sem("s_ctx")
        s_x = [sem(f"s_x{j}") for j in range(NCH)]
        s_ident, s_pfill = sem("s_ident"), sem("s_pfill")
        s_stat, s_var, s_sd, s_xn = sem("s_stat"), sem("s_var"), sem("s_sd"), sem("s_xn")
        s_chain = sem("s_chain")
        s_job = sem("s_job")
        s_high, s_rest, s_mid, s_low = sem("s_high"), sem("s_rest"), sem("s_mid"), sem("s_low")
        s_xT, s_v, s_vzero, s_vone = sem("s_xT"), sem("s_v"), sem("s_vzero"), sem("s_vone")
        s_kout = [sem(f"s_kout{mt}") for mt in range(DT)]
        s_qout = [[sem(f"s_qout{j}_{mt}") for mt in range(DT)] for j in range(NCH)]
        s_kin = [sem(f"s_kin{n}") for n in range(3)]
        s_qin = [sem(f"s_qin{mt}") for mt in range(DT)]
        s_qmore = sem("s_qmore")
        s_score, s_prob, s_av, s_vcur = sem("s_score"), sem("s_prob"), sem("s_av"), sem("s_vcur")
        s_slot, s_free = sem("s_slot"), sem("s_free")
        s_cmax, s_csplit, s_cpart, s_crow = (sem("s_cmax"), sem("s_csplit"),
                                                     sem("s_cpart"), sem("s_crow"))
        s_osb, s_den, s_rden, s_rrow = sem("s_osb"), sem("s_den"), sem("s_rden"), sem("s_rrow")
        s_acc, s_wo, s_wozero, s_rt = sem("s_acc"), sem("s_wo"), sem("s_wozero"), sem("s_rt")
        s_proj, s_resid, s_n2, s_turn2 = sem("s_proj"), sem("s_resid"), sem("s_n2"), sem("s_turn2")
        s_h2, s_l2, s_rt2, s_route = sem("s_h2"), sem("s_l2"), sem("s_rt2"), sem("s_route")
        s_lraw, s_lrows, s_logit, s_lread = sem("s_lraw"), sem("s_lrows"), sem("s_logit"), sem("s_lread")
        s_shift, s_exp, s_iota = sem("s_shift"), sem("s_exp"), sem("s_iota")
        s_wraw, s_whi, s_wlo = sem("s_wraw"), sem("s_whi"), sem("s_wlo")
        s_gate, s_up, s_silu, s_prod = sem("s_gate"), sem("s_up"), sem("s_silu"), sem("s_prod")
        s_fhi, s_flo, s_down, s_sum, s_out = sem("s_fhi"), sem("s_flo"), sem("s_down"), sem("s_sum"), sem("s_out")

        kparts = nc.dram_tensor("kparts", [DT, 3, P, KEYS], BF16, kind="Internal").ap()
        qparts = nc.dram_tensor("qparts", [NCH, DT, 3, P, CHUNK], BF16, kind="Internal").ap()

        block = stack.enter_context(nc.Block())

        def prologue_slots():
            ahead = [("max", 1, i) for i in range(AHEAD)]
            return [("max", 0, i) for i in range(64)] + ahead[:TURN_LAG] + [("turn", 0, 0)] + ahead[TURN_LAG:]

        KC = [(k, min(CHUNK, KEYS - k)) for k in range(0, KEYS, CHUNK)]
        def turn_jobs(j):
            return [("T", j, dt) for dt in range(DT)]

        def query_jobs(j):
            return [("Q", j, mt) for mt in range(DT)]

        def key_jobs(mt):
            return [("K", mt, kc) for kc in range(len(KC))]

        norm = lambda j: [("N", j, 0), ("M", j, 0)]
        keys0 = key_jobs(0)
        early = (norm(0) + keys0[:1] + turn_jobs(0) + keys0[1:] + [("Q", 0, 0)] + norm(1) + [("Q", 0, 1)]
                 + key_jobs(1))
        late = turn_jobs(1) + query_jobs(1)
        for j in range(2, NCH):
            late += norm(j) + turn_jobs(j) + query_jobs(j)
        values_from = 46
        late_values = [("V", kt, 0) for kt in range(KT)]
        opening = list(early)
        for n, what in enumerate(prologue_slots()):
            opening.append(what)
            if n % 2:
                if late:
                    opening.append(late.pop(0))
                elif late_values and n >= values_from:
                    opening.append(late_values.pop(0))
        assert not late and not late_values
        jobs = [job for job in opening if job[0] in "KTQV"]
        number = {job: n for n, job in enumerate(jobs)}
        splits = [job for job in jobs if job[0] in "KQ"]
        nth_split = {job: n for n, job in enumerate(splits)}
        turns = [job for job in jobs if job[0] == "T"]
        nth_turn = {job: n for n, job in enumerate(turns)}

        def part(job, p):
            kind, a, b = job
            if kind == "K":
                k0, n = KC[b]
                return Kp[:, a, p, k0:k0 + n]
            return Qp[:, b, p, a * CHUNK:(a + 1) * CHUNK]

        def width(job):
            return KC[job[2]][1] if job[0] == "K" else CHUNK

        def emptied(eng, job):
            if job[0] in "KQ":
                eng.wait_ge(s_rest, nth_split[job] + 1)
            elif job[0] == "T":
                eng.wait_ge(s_xT, nth_turn[job] + 1)
            else:
                eng.wait_ge(s_v, job[1] + 1)

        def keys_of(t):
            return P if t < KT - 1 else LASTK

        def group_of(v):
            return v % G

        def slot_base(v):
            if isinstance(v, int) and v == 0:
                return PRO_SLOTS
            if isinstance(v, int) and v == UNITS - 1:
                return PRO_SLOTS - 1 + (UNITS - 1) * SLOTS - AHEAD
            return v * SLOTS + (PRO_SLOTS - 1)

        def bank_of(v, i):
            first = PRO_SLOTS if isinstance(v, int) and v == 0 else (
                slot_base(v) if isinstance(v, int) else PRO_SLOTS - 1)
            return MAX_BANKS[(first + i) % 3]

        def normalised(eng, u):
            if isinstance(u, int) and u >= UNITS - 2:
                eng.wait_ge(s_free, slot_base(UNITS - 1) + 1 + (u - (UNITS - 2)))
            else:
                eng.wait_ge(s_free, slot_base(u + 1) + (NORM_SLOT + 1))

        def turned(u):
            if isinstance(u, int) and u == 0:
                return 64 + TURN_LAG + 1
            lag = 0 if isinstance(u, int) and u == UNITS - 1 else TURN_LAG
            return (u - 1) * SLOTS + (PRO_SLOTS - 1 + 64 - AHEAD + 1 + lag + 1)

        def each_unit(eng, body):
            body(0, 0)
            with eng.Fori(0, (UNITS - 4) // 2) as pair:
                body(pair * 2 + 1, 1)
                body(pair * 2 + 2, 0)
            for v in range(UNITS - 3, UNITS):
                body(v, v % 2)

        def piece(i):
            c, qt, q = i // 16, i // 4 % 4, i % 4
            return c, qt, q * STEP, STEP if q < 3 else KEYS - 3 * STEP

        def steps(eng, step):
            step(0, 1)
            with eng.Fori(0, E // 2 - 1) as i:
                for k in range(2, 10):
                    step(i, k)
            for k in range(2, 8):
                step(E // 2 - 1, k)

        TOTAL_SLOTS = slot_base(UNITS - 1) + 1
        LAST_BANK, TURN_BANKS = 7, (5, 6)
        LOGIT_BANKS, ROUTE_BANK = (7, O_BANK), 5

        @block.sync
        def _(sp):
            xv = x.rearrange("(j q p) d -> j p q d", j=NCH, p=P)
            sp.dma_start(xt[:, 0], xv[0]).then_inc(s_x[0], 16)
            sp.dma_start(wkv[:], WkvT).then_inc(s_wkv, 16)
            sp.dma_start(ctx_sb[:], ctxT).then_inc(s_ctx, 16)
            sp.dma_start(wq[:], WqT.rearrange("(t p) n -> p t n", p=P)).then_inc(s_wq, 16)
            for j in range(1, NCH):
                sp.dma_start(xt[:, j], xv[j]).then_inc(s_x[j], 16)
            sp.dma_start(rt[:], router.rearrange("(t p) e -> p t e", p=P)).then_inc(s_rt, 16)

            Kv = Kst[:].rearrange("p (h k) -> p h k", k=KPAD)
            Qv = Qst[:].rearrange("p (j h i) -> p j h i", j=NCH, i=CHUNK)

            def keys_out(mt):
                sp.wait_ge(s_low, nth_split[("K", mt, len(KC) - 1)] + 1)
                sp.dma_start(kparts[mt].rearrange("a p k -> p a k"), Kp[:, mt, :, 0:KEYS]).then_inc(s_kout[mt], 16)

            def keys_in(mt, h0, h1, done):
                sp.wait_ge(s_kout[mt], 16)
                for b in range(BLOCKS):
                    sp.dma_start(Kv[b * HD:(b + 1) * HD, mt * MT_HEADS + h0:mt * MT_HEADS + h1, 0:KEYS],
                                 kparts[mt, K_PARTS[b], h0 * HD:h1 * HD].rearrange(
                                     "(h d) k -> d h k", d=HD)).then_inc(done, 16)

            def queries_out(j, mt):
                sp.wait_ge(s_low, nth_split[("Q", j, mt)] + 1)
                sp.dma_start(qparts[j, mt].rearrange("a p i -> p a i"),
                             Qp[:, mt, :, j * CHUNK:(j + 1) * CHUNK]).then_inc(s_qout[j][mt], 16)

            def queries_in(j, mt, done):
                sp.wait_ge(s_qout[j][mt], 16)
                for b in range(BLOCKS):
                    sp.dma_start(Qv[b * HD:(b + 1) * HD, j, mt * MT_HEADS:(mt + 1) * MT_HEADS, :],
                                 qparts[j, mt, Q_PARTS[b]].rearrange("(h d) i -> d h i", d=HD)).then_inc(done, 16)

            keys_out(0)
            queries_out(0, 0)
            keys_in(0, 0, HPG, s_kin[0])
            queries_in(0, 0, s_qin[0])
            keys_in(0, HPG, MT_HEADS, s_kin[1])
            queries_out(0, 1)
            keys_out(1)
            queries_in(0, 1, s_qin[1])
            keys_in(1, 0, MT_HEADS, s_kin[2])
            for j in range(1, NCH):
                for mt in range(DT):
                    queries_out(j, mt)
                for mt in range(DT):
                    queries_in(j, mt, s_qmore)

            def send_crow(v):
                sp.wait_ge(s_cpart, v + 1)
                for p in range(3):
                    row = Qst[ROWS + p:ROWS + p + 1, bass.ds(v * (HPG * CHUNK), HPG * CHUNK)]
                    sp.dma_start(row.rearrange("o (t i) -> o t i", i=P), cpart[:, p, :]).then_inc(s_crow, 16)

            def spread_den(v):
                sp.wait_ge(s_osb, v + 1)
                sp.dma_start(den[:], osb[0:P:QUAD, :].rearrange("c (e i) -> c e i", e=QUAD // HPG)).then_inc(s_den, 16)
                sp.wait_ge(s_rden, v + 1)
                if positive(v):
                    normalised(sp, v - 1)
                sp.dma_start(rrow[:].rearrange("c (e i) -> c e i", e=QUAD // HPG), rden[:]).then_inc(s_rrow, 16)

            send_crow(0)

            def body(v, odd):
                if positive(v):
                    spread_den(v - 1)
                if isinstance(v, int) and v == UNITS - 2:
                    sp.wait_ge(s_score, (UNITS - 2) * KT * HPG)
                    sp.dma_start(acc[:], x.rearrange("(n p) d -> p n d", p=P)).then_inc(s_acc, 16)
                    sp.wait_ge(s_wozero, 1)
                    for c in range(HPG):
                        sp.dma_start(wo[c * QUAD + 1:c * QUAD + 1 + HD, :, :],
                                     WoT.rearrange("(g c d) n -> c d g n", g=G, c=HPG)[c]).then_inc(s_wo, 16)
                    load_expert(0)
                if not isinstance(v, int) or v + 1 < UNITS:
                    send_crow(v + 1)

            def load_expert(e):
                if positive(e):
                    sp.wait_ge(s_wlo, e)
                sp.dma_start(wraw[:, 0].rearrange("p (t f) -> p t f", f=F),
                             gating.rearrange("e (t p) f -> p (e t) f", p=P)[:, bass.ds(e * DT, DT), :]).then_inc(s_wraw, 16)
                sp.dma_start(wraw[:, 1].rearrange("p (t f) -> p t f", f=F),
                             up.rearrange("e (t p) f -> p (e t) f", p=P)[:, bass.ds(e * DT, DT), :]).then_inc(s_wraw, 16)
                sp.dma_start(wraw[:, 2].rearrange("p (t n) -> p t n", n=D),
                             down.rearrange("e (t p) n -> p (e t) n", p=P)[:, bass.ds(e * FT, FT), :]).then_inc(s_wraw, 16)

            each_unit(sp, body)
            spread_den(UNITS - 1)
            with sp.Fori(1, E) as e:
                load_expert(e)
            for j in range(NCH):
                sp.wait_ge(s_sum, (E - 1) * NTILES + (j + 1) * QT)
                sp.dma_start(out.rearrange("(j q p) d -> j p q d", j=NCH, p=P)[j],
                             acc[:, j * QT:(j + 1) * QT, :]).then_inc(s_out, 16)
            sp.wait_ge(s_out, 16 * NCH)

        @block.gpsimd
        def _(pool):
            pool.memset(ident[:], 0.0).then_inc(s_pfill, 1)
            pool.wait_ge(s_pfill, 1)
            pool.affine_select(out=ident[:], in_=ident[:], compare_op=ALU.not_equal, fill=1.0, base=0,
                               pattern=[[-1, P]], channel_multiplier=1).then_inc(s_ident, 1)
            pool.memset(zeros[:], 0.0).then_inc(s_iota, 1)
            pool.memset(select[:], 1.0).then_inc(s_pfill, 1)
            pool.wait_ge(s_pfill, 2)
            pool.affine_select(out=select[:], in_=select[:], compare_op=ALU.is_ge, fill=0.0, base=0,
                               pattern=[[1, P]], channel_multiplier=-QUAD).then_inc(s_pfill, 1)
            pool.wait_ge(s_pfill, 3)
            pool.affine_select(out=select[:], in_=select[:], compare_op=ALU.is_ge, fill=0.0, base=QUAD - 1,
                               pattern=[[-1, P]], channel_multiplier=QUAD).then_inc(s_ident, 1)
            two_ones = struct.unpack("<f", struct.pack("<I", 0x3F803F80))[0]
            pool.wait_ge(s_ident, 2)
            pool.memset(Kst[ROWS:CROWS, :].bitcast(F32), two_ones).then_inc(s_ident, 1)
            pool.wait_ge(s_ident, 3)

            def low(n):
                w = width(splits[n])
                pool.wait_ge(s_mid, n + 1)
                pool.tensor_tensor(part(splits[n], 2), rest[n % 2][:, 0:w], part(splits[n], 1),
                                   ALU.subtract).then_inc(s_low, 1)

            def clear_v(n, g0, g1):
                cols = V[:, g0 * KT * P:g1 * KT * P]
                pool.memset(cols, 0.0).then_inc(s_vzero, 1)
                pool.wait_ge(s_vzero, n)
                pool.memset(cols.rearrange("p (n w) -> p n w", w=QUAD)[:, :, 0:1], 1.0).then_inc(s_vone, 1)

            for n, job in enumerate(splits):
                low(n)
                if job == ("Q", 1, 1):
                    for mt in range(DT):
                        pool.wait_ge(s_kout[mt], 16)
                    clear_v(1, 0, 2)
            for k in range(E):
                pool.memset(iota[:, :, k:k + 1], float(k)).then_inc(s_iota, 1)
            pool.wait_ge(s_job, number[("Q", NCH - 1, DT - 1)] + 1)
            clear_v(2, 2, G)

            def copy_v(v, kt):
                n = keys_of(kt)
                if positive(v):
                    pool.wait_ge(s_av, v * KT + (kt + 1 - KT))
                pool.wait_ge(s_v, KT)
                pool.tensor_copy(Vcur[0:n, kt, :],
                                 V[0:n, bass.ds(group_of(v) * (KT * P) + kt * P, P)]).then_inc(s_vcur, 1)

            def split_c(v):
                pool.wait_ge(s_iota, 1)
                pool.wait_ge(s_free, turned(v))
                if positive(v):
                    pool.wait_ge(s_crow, v * 48)
                pool.tensor_tensor(cpart[:, 0, :], negc[:], zeros[0:16, 0].to_broadcast([16, P]), ALU.add).then_inc(s_csplit, 1)
                pool.wait_ge(s_csplit, v * 4 + 1)
                pool.tensor_tensor(crest[:], negc[:], cpart[:, 0, :], ALU.subtract).then_inc(s_csplit, 1)
                pool.wait_ge(s_csplit, v * 4 + 2)
                pool.tensor_tensor(cpart[:, 1, :], crest[:], zeros[0:16, 0].to_broadcast([16, P]), ALU.add).then_inc(s_csplit, 1)
                pool.wait_ge(s_csplit, v * 4 + 3)
                pool.tensor_tensor(negc[:], crest[:], cpart[:, 1, :], ALU.subtract).then_inc(s_csplit, 1)
                pool.wait_ge(s_csplit, v * 4 + 4)
                pool.tensor_tensor(cpart[:, 2, :], negc[:], zeros[0:16, 0].to_broadcast([16, P]), ALU.add).then_inc(s_cpart, 1)

            pool.wait_ge(s_v, KT)
            for kt in range(KT // 2):
                copy_v(0, kt)
            split_c(0)
            for kt in range(KT // 2, KT):
                copy_v(0, kt)

            def split_expert(e, half):
                pool.wait_ge(s_wraw, e * 48 + 48)
                if not isinstance(e, int):
                    pool.wait_ge(s_down, e * NTILES - NTILES)
                elif e == 1:
                    pool.wait_ge(s_score, UNITS * KT * HPG)
                pool.tensor_tensor(w_hi[half][:], wraw[:], zeros[:].to_broadcast([P, 3, FT * D]),
                                   ALU.add).then_inc(s_whi, 1)
                pool.wait_ge(s_whi, e + 1)
                pool.tensor_tensor(w_lo[half][:], wraw[:], w_hi[half][:].bitcast(F32),
                                   ALU.subtract).then_inc(s_wlo, 1)

            def body(v, odd):
                if isinstance(v, int) and v == UNITS - 2:
                    pool.wait_ge(s_score, (UNITS - 2) * KT * HPG)
                    pool.memset(wo[:], 0.0).then_inc(s_wozero, 1)
                if isinstance(v, int) and v == UNITS - 1:
                    return
                for kt in range(KT):
                    if kt == SPLIT_AT:
                        split_c(v + 1)
                    copy_v(v + 1, kt)

            each_unit(pool, body)
            split_expert(0, 0)
            split_expert(1, 1)
            with pool.Fori(1, E // 2) as i:
                split_expert(i * 2, 0)
                split_expert(i * 2 + 1, 1)

        @block.scalar
        def _(act):
            def deviation(j):
                act.wait_ge(s_var, j + 1)
                act.activation(sd[:], ve[:], ACT.Sqrt).then_inc(s_sd, 1)

            def high(job):
                n = nth_split[job]
                act.wait_ge(s_job, number[job] + 1)
                act.copy(part(job, 0), ps[:, number[job] % JOB_BANKS, 0:width(job)]).then_inc(s_high, 1)

            def turned(job):
                _, j, dt = job
                act.wait_ge(s_job, number[job] + 1)
                if j >= 2:
                    act.wait_ge(s_job, number[("Q", j - 2, DT - 1)] + 1)
                act.copy(xnT[j % 2][:, dt, :], ps[:, number[job] % JOB_BANKS, :]).then_inc(s_xT, 1)

            def values(kt):
                n = keys_of(kt)
                job = number[("V", kt, 0)]
                act.wait_ge(s_job, job + 1)
                act.copy(V[0:n, :].rearrange("p (g k c w) -> p k g c w", g=G, k=KT, c=HPG)[:, kt, :, :, 1:1 + HD],
                         ps[0:n, job % JOB_BANKS, 0:D].rearrange("p (g c d) -> p g c d", g=G, c=HPG)).then_inc(s_v, 1)

            def middle(n):
                w = width(splits[n])
                act.wait_ge(s_rest, n + 1)
                act.copy(part(splits[n], 1), rest[n % 2][:, 0:w]).then_inc(s_mid, 1)

            at_once = (("K", 0, len(KC) - 1), ("Q", 0, 0), ("Q", 1, 1), splits[-1])
            for job in opening:
                if job[0] == "N":
                    deviation(job[1])
                elif job[0] == "T":
                    turned(job)
                elif job[0] == "V":
                    if job[1] == 0:
                        act.wait_ge(s_vone, 2)
                    values(job[1])
                elif job[0] in "KQ":
                    high(job)
                    if nth_split[job] and splits[nth_split[job] - 1] not in at_once:
                        middle(nth_split[job] - 1)
                    if job in at_once:
                        middle(nth_split[job])

            def exp(v, t, c, odd):
                n = keys_of(t)
                act.wait_ge(s_score, v * (KT * HPG) + (t * HPG + c + 1))
                if c == 0:
                    used = v * KT + (t - 1)
                    if positive(used):
                        act.wait_ge(s_av, used)
                act.activation(probs[0:n, (t + odd) % 2, c, :], ps[0:n, c, :], ACT.Exp, scale=SCALE).then_inc(s_prob, 1)

            def take_output(v):
                act.wait_ge(s_av, v * KT + KT)
                if positive(v):
                    normalised(act, v - 1)
                act.copy(osb[:], ps[:, O_BANK, :]).then_inc(s_osb, 1)

            def body(v, odd):
                for t in range(KT):
                    for c in range(HPG):
                        exp(v, t, c, odd)
                    if t == 0 and positive(v):
                        take_output(v - 1)

            each_unit(act, body)
            take_output(UNITS - 1)

            def high2(j):
                for dt in range(DT):
                    act.wait_ge(s_turn2, j * DT + dt + 1)
                    act.copy(x2_hi[:, dt, j * CHUNK:(j + 1) * CHUNK], ps[:, TURN_BANKS[dt], :]).then_inc(s_h2, 1)

            for j in range(NCH):
                deviation(NCH + j)
                if j:
                    high2(j - 1)

            def hidden(i, k):
                n = i * 8 + k
                for f in range(FT):
                    idx = n * FT + f
                    act.wait_ge(s_gate, idx + 1)
                    if positive(idx - 1):
                        act.wait_ge(s_prod, idx - 1)
                    act.activation(silu[:, f % 2, :], ps[:, 2 * (f % 2), :], ACT.Silu).then_inc(s_silu, 1)
                    act.wait_ge(s_prod, idx + 1)
                    if positive(n - 1):
                        act.wait_ge(s_down, n * QT - QT)
                    act.copy(f_hi[k % 2][:, f, :], prod[:, f % 2, :]).then_inc(s_fhi, 1)

            def step(i, k):
                hidden(i, k)
                if isinstance(i, int) and i == 0 and k == 1:
                    take_logits(3)
                    act.wait_ge(s_shift, 1)
                    act.activation(prob[:], work[:], ACT.Exp).then_inc(s_exp, 1)
                    act.wait_ge(s_shift, 2)
                    act.activation(total[:], pick[:], ACT.Exp).then_inc(s_exp, 1)

            def take_logits(j):
                act.wait_ge(s_lraw, j + 1)
                act.copy(lrows[:, j, :], ps[0:2 * E, LOGIT_BANKS[j % 2], :]).then_inc(s_lrows, 1)

            take_logits(0)
            take_logits(1)
            hidden(0, 0)
            high2(NCH - 1)
            take_logits(2)
            steps(act, step)

        @block.vector
        def _(dve):
            links = [0]

            def link(instruction):
                links[0] += 1
                instruction.then_inc(s_chain, 1)
                dve.wait_ge(s_chain, links[0])

            def norm_stats(k, src):
                for q in range(QT):
                    dve.bn_stats(stats[:, q, :], src(q)).then_inc(s_stat, 1)
                dve.wait_ge(s_stat, k * 2 * QT + QT)
                for q in range(QT):
                    dve.bn_aggr(mv[:, q, :], stats[:, q, :]).then_inc(s_stat, 1)
                dve.wait_ge(s_stat, (k + 1) * 2 * QT)
                dve.tensor_scalar(ve[:], mv[:, :, 1], LN_EPS, None, ALU.add).then_inc(s_var, 1)

            def norm_rows(k, src, dst):
                dve.wait_ge(s_sd, k + 1)
                link(dve.reciprocal(rs[:], sd[:]))
                link(dve.tensor_tensor(nt[:], rs[:], rs[:], ALU.mult))
                link(dve.tensor_tensor(nt[:], nt[:], ve[:], ALU.mult))
                link(dve.tensor_scalar(nt[:], nt[:], -0.5, 1.5, ALU.mult, ALU.add))
                link(dve.tensor_tensor(rs[:], rs[:], nt[:], ALU.mult))
                for q in range(QT):
                    last = dve.tensor_scalar(dst(q), src(q), mv[:, q, 0:1], rs[:, q:q + 1],
                                             ALU.subtract, ALU.mult)
                    if q < QT - 1:
                        last.then_inc(s_chain, 1)
                        links[0] += 1
                return last

            def stats1(j):
                dve.wait_ge(s_x[j], 16)
                norm_stats(j, lambda q: xt[:, j, q, :])

            def norm1(j):
                norm_rows(j, lambda q: xt[:, j, q, :], lambda q: xt[:, j, q, :]).then_inc(s_xn, 1)

            def split(job):
                n, w = nth_split[job], width(job)
                dve.wait_ge(s_high, n + 1)
                if n >= 2:
                    dve.wait_ge(s_low, n - 1)
                dve.tensor_tensor(rest[n % 2][:, 0:w], ps[:, number[job] % JOB_BANKS, 0:w], part(job, 0),
                                  ALU.subtract).then_inc(s_rest, 1)

            def slot(v, count, bank, what, u):
                kind, _, i = what
                dve.wait_ge(s_slot, count)
                if kind == "max":
                    n = piece(i)[3]
                    dve.tensor_reduce(mx[:, i:i + 1], ps[:, bank, 0:n], AX.X, ALU.max).then_inc(s_free, 1)
                elif kind == "turn":
                    if positive(u):
                        dve.wait_ge(s_cpart, u)
                    dve.tensor_scalar(negc[:], ps[0:16, bank, 0:P], -1.0, None, ALU.mult).then_inc(s_free, 1)
                else:
                    dve.tensor_tensor(OT[:, bass.ds(u * CHUNK, CHUNK)], osb[:], ps[:, bank, :],
                                      ALU.mult).then_inc(s_free, 1)

            def row_max(u, count):
                dve.wait_ge(s_free, count)
                dve.tensor_reduce(cmax[:], mx[:].rearrange("p (a b) -> p a b", b=4), AX.X,
                                  ALU.max).then_inc(s_cmax, 1)
                dve.wait_ge(s_cmax, u + 1)

            def invert(u):
                dve.wait_ge(s_den, u * 16 + 16)
                if positive(u):
                    dve.wait_ge(s_rrow, u * 16)
                dve.reciprocal(rden[:], den[:]).then_inc(s_rden, 1)

            n = 0
            waiting = []
            for step_no, what in enumerate(opening):
                while waiting and (waiting[0][0] <= step_no or what[0] in "NM" and n == 0):
                    split(waiting.pop(0)[1])
                if what[0] == "N":
                    stats1(what[1])
                elif what[0] == "M":
                    norm1(what[1])
                    if what[1] == NCH - 1:
                        dve.wait_ge(s_rt, 16)
                        link(dve.tensor_copy(rt2[:, :, 0:E], rt[:]))
                        dve.tensor_tensor(rt2[:, :, E:2 * E], rt[:], rt2[:, :, 0:E].bitcast(F32),
                                          ALU.subtract).then_inc(s_rt2, 1)
                elif what[0] in "KQ":
                    waiting.append((step_no + (3 if n else 0), what))
                elif what[0] in ("max", "turn"):
                    slot(0, n + 1, MAX_BANKS[n % 3], what, what[1])
                    n += 1
                    if what == ("max", 0, 63):
                        row_max(0, n)

            def body(v, odd):
                first = slot_base(v)
                n = 0
                for i, what in enumerate(slots_of(v, UNITS)):
                    if i == RECIP_SLOT and positive(v):
                        invert(v - 1)
                    if what is None:
                        continue
                    slot(v, first + (n + 1), bank_of(v, n), what, v + what[1])
                    n += 1
                    if what == ("max", 1, 63):
                        row_max(v + 1, first + n)

            each_unit(dve, body)

            def residual(j):
                for q in range(QT):
                    n = j * QT + q
                    dve.wait_ge(s_proj, n + 1)
                    dve.tensor_tensor(acc[:, n, :], ps[:, n % 4, 0:D], acc[:, n, :], ALU.add).then_inc(s_resid, 1)
                dve.wait_ge(s_resid, (j + 1) * QT)
                if j >= 2:
                    dve.wait_ge(s_turn2, (j - 1) * DT)
                norm_stats(NCH + j, lambda q: acc[:, j * QT + q, :])
                norm_rows(NCH + j, lambda q: acc[:, j * QT + q, :], lambda q: xn2[:, j % 2, q, :]).then_inc(s_n2, 1)

            def low2(j):
                for dt in range(DT):
                    cols = slice(j * CHUNK, (j + 1) * CHUNK)
                    dve.wait_ge(s_h2, j * DT + dt + 1)
                    dve.tensor_tensor(x2_lo[:, dt, cols], ps[:, TURN_BANKS[dt], :],
                                      x2_hi[:, dt, cols].bitcast(F32), ALU.subtract).then_inc(s_l2, 1)

            dve.wait_ge(s_acc, 16)
            residual(0)
            invert(UNITS - 1)
            residual(1)
            low2(0)
            dve.wait_ge(s_slot, TOTAL_SLOTS + 1)
            dve.tensor_tensor(OT[:, (UNITS - 1) * CHUNK:UNITS * CHUNK], osb[:], ps[:, LAST_BANK, :],
                              ALU.mult).then_inc(s_free, 1)
            residual(2)
            low2(1)
            residual(3)
            low2(2)

            def product(i, k):
                n = i * 8 + k
                for f in range(FT):
                    idx = n * FT + f
                    dve.wait_ge(s_up, idx + 1)
                    dve.wait_ge(s_silu, idx + 1)
                    if positive(idx - 1):
                        dve.wait_ge(s_fhi, idx - 1)
                    dve.tensor_tensor(prod[:, f % 2, :], silu[:, f % 2, :], ps[:, 2 * (f % 2) + 1, :],
                                      ALU.mult).then_inc(s_prod, 1)
                    dve.wait_ge(s_fhi, idx + 1)
                    dve.tensor_tensor(f_lo[k % 2][:, f, :], prod[:, f % 2, :], f_hi[k % 2][:, f, :].bitcast(F32),
                                      ALU.subtract).then_inc(s_flo, 1)

            def add_up(i, k):
                n = i * 8 + k
                e = i * 2 + k // 4
                for q in range(QT):
                    tile = k % 4 * QT + q
                    dve.wait_ge(s_down, n * QT + (q + 1))
                    dve.scalar_tensor_tensor(acc[:, tile, :], ps[:, 4 + q, 0:D],
                                             weight[:, bass.ds(e * NTILES + tile, 1)], acc[:, tile, :],
                                             op0=ALU.mult, op1=ALU.add).then_inc(s_sum, 1)

            def step(i, k):
                product(i, k)
                if isinstance(i, int) and i == 0 and k == 1:
                    route()
                add_up(i, k - 1)

            def route():
                wide = lambda a: a[:].to_broadcast(W8)
                lv = ps[:, ROUTE_BANK, 0:NTILES * 2 * E].rearrange("p (n w) -> p n w", w=2 * E)
                dve.wait_ge(s_logit, 1)
                link(dve.tensor_copy(logit[:], lv[:, :, 0:E]))
                dve.tensor_tensor(logit[:], logit[:], lv[:, :, E:2 * E], ALU.add).then_inc(s_lread, 1)
                dve.wait_ge(s_lread, 1)
                link(dve.tensor_reduce(top1[:], logit[:], AX.X, ALU.max))
                dve.tensor_tensor(work[:], logit[:], wide(top1), ALU.subtract).then_inc(s_shift, 1)
                dve.wait_ge(s_exp, 1)
                link(dve.tensor_reduce(total[:], prob[:], AX.X, ALU.add))
                link(dve.reciprocal(pick[:], total[:]))
                link(dve.tensor_tensor(prob[:], prob[:], wide(pick), ALU.mult))

                def first_largest(top, hot):
                    link(dve.tensor_reduce(top[:], prob[:], AX.X, ALU.max))
                    link(dve.tensor_tensor(hot[:], prob[:], wide(top), ALU.is_equal))
                    link(dve.scalar_tensor_tensor(work[:], hot[:], -float(E), iota[:], op0=ALU.mult, op1=ALU.add))
                    link(dve.tensor_reduce(pick[:], work[:], AX.X, ALU.min))
                    link(dve.tensor_tensor(hot[:], work[:], wide(pick), ALU.is_equal))

                dve.wait_ge(s_iota, 1 + E)
                first_largest(top1, hot1)
                link(dve.scalar_tensor_tensor(prob[:], hot1[:], -2.0, prob[:], op0=ALU.mult, op1=ALU.add))
                first_largest(top2, hot2)
                dve.tensor_tensor(pick[:], top2[:], top1[:], ALU.subtract).then_inc(s_shift, 1)
                dve.wait_ge(s_exp, 2)
                link(dve.tensor_scalar(top1[:], total[:], 1.0, None, ALU.add))
                link(dve.reciprocal(top1[:], top1[:]))
                link(dve.tensor_tensor(top2[:], total[:], top1[:], ALU.mult))
                link(dve.tensor_tensor(hot1[:], hot1[:], wide(top1), ALU.mult))
                link(dve.tensor_tensor(hot2[:], hot2[:], wide(top2), ALU.mult))
                dve.tensor_tensor(weight[:].rearrange("p (e n) -> p n e", n=NTILES), hot1[:], hot2[:],
                                  ALU.add).then_inc(s_route, 1)
                dve.wait_ge(s_route, 1)

            product(0, 0)
            low2(NCH - 1)
            steps(dve, step)
            add_up(E // 2 - 1, 7)

        @block.tensor
        def _(pe):
            pe.wait_ge(s_wkv, 16)
            pe.wait_ge(s_ctx, 16)
            def fill(job):
                n, (kind, a, b) = number[job], job
                bank = ps[:, n % JOB_BANKS, :]
                if n >= JOB_BANKS:
                    emptied(pe, jobs[n - JOB_BANKS])
                if kind == "K":
                    k0, w = KC[b]
                    pe.matmul(bank[:, 0:w], wkv[:, a * P:(a + 1) * P], ctx_sb[:, k0:k0 + w],
                              start=True, stop=True).then_inc(s_job, 1)
                elif kind == "T":
                    pe.wait_ge(s_ident, 1)
                    pe.wait_ge(s_xn, a + 1)
                    for q in range(QT):
                        mm = pe.transpose(bank[:, q * P:(q + 1) * P], xt[:, a, q, b * P:(b + 1) * P], ident[:])
                    mm.then_inc(s_job, 1)
                elif kind == "Q":
                    pe.wait_ge(s_wq, 16)
                    pe.wait_ge(s_xT, (a + 1) * DT)
                    for dt in range(DT):
                        mm = pe.matmul(bank, wq[:, dt, b * P:(b + 1) * P], xnT[a % 2][:, dt, :],
                                       start=(dt == 0), stop=(dt == DT - 1))
                    mm.then_inc(s_job, 1)
                else:
                    w = keys_of(a)
                    pe.matmul(bank[0:w, 0:D], ctx_sb[:, a * P:a * P + w], wkv[:, D:2 * D],
                              start=True, stop=True).then_inc(s_job, 1)

            def slot(v, before, bank, what, u):
                kind, _, i = what
                if positive(before - 2):
                    pe.wait_ge(s_free, before - 2)
                if kind == "max":
                    c, qt, k0, n = piece(i)
                    g = group_of(u)
                    pe.matmul(ps[:, bank, 0:n],
                              Qst[0:ROWS, bass.ds(u * (HPG * CHUNK) + (c * CHUNK + qt * P), P)],
                              Kst[0:ROWS, bass.ds(g * (HPG * KPAD) + (c * KPAD + k0), n)],
                              start=True, stop=True).then_inc(s_slot, 1)
                elif kind == "turn":
                    pe.wait_ge(s_cmax, u + 1)
                    pe.transpose(ps[0:16, bank, 0:P], cmax[:], ident[:]).then_inc(s_slot, 1)
                else:
                    pe.wait_ge(s_rrow, u * 16 + 16)
                    pe.matmul(ps[:, bank, :], select[:], rrow[:], start=True, stop=True).then_inc(s_slot, 1)

            def stacked(g):
                pe.wait_ge(s_kin[min(g, 2)], BLOCKS * 16)
                pe.wait_ge(s_qin[g // 2], BLOCKS * 16)

            n = 0
            for what in opening:
                if what[0] in ("max", "turn"):
                    if n == 0:
                        stacked(0)
                    if what == ("max", 1, 0):
                        stacked(1)
                    slot(0, n, MAX_BANKS[n % 3], what, what[1])
                    n += 1
                elif what[0] not in "NM":
                    fill(what)
            for job in jobs[-JOB_BANKS:]:
                emptied(pe, job)

            def score(v, t, c):
                n = keys_of(t)
                g = group_of(v)
                done = v * (KT * HPG) + (t * HPG + c + 1 - HPG)
                if positive(done):
                    pe.wait_ge(s_prob, done)
                pe.matmul(ps[0:n, c, :],
                          Kst[0:CROWS, bass.ds(g * (HPG * KPAD) + (c * KPAD + t * P), n)],
                          Qst[0:CROWS, bass.ds(v * (HPG * CHUNK) + c * CHUNK, CHUNK)],
                          start=True, stop=True).then_inc(s_score, 1)

            def attend(v, t, odd):
                n = keys_of(t)
                pe.wait_ge(s_prob, v * (KT * HPG) + (t * HPG + HPG))
                pe.wait_ge(s_vcur, v * KT + (t + 1))
                if t == 0 and positive(v):
                    pe.wait_ge(s_osb, v)
                for c in range(HPG):
                    mm = pe.matmul(ps[c * QUAD:(c + 1) * QUAD, O_BANK, :], Vcur[0:n, t, c * QUAD:(c + 1) * QUAD],
                                   probs[0:n, (t + odd) % 2, c, :], start=(t == 0), stop=(t == KT - 1))
                mm.then_inc(s_av, 1)

            def body(v, odd):
                first = slot_base(v)
                todo = list(enumerate(slots_of(v, UNITS)))
                n = [0]

                def next_slot():
                    if not todo:
                        return
                    _, what = todo.pop(0)
                    if what is None:
                        return
                    if isinstance(v, int) and v == 0 and what == ("max", 2, 0):
                        stacked(2)
                    slot(v, first + n[0], bank_of(v, n[0]), what, v + what[1])
                    n[0] += 1

                if isinstance(v, int) and v == 0:
                    pe.wait_ge(s_ident, 3)
                pe.wait_ge(s_crow, v * 48 + 48)
                for t in range(KT):
                    for c in range(HPG):
                        score(v, t, c)
                        next_slot()
                    if t:
                        attend(v, t - 1, odd)
                    elif positive(v):
                        attend(v - 1, KT - 1, 1 - odd)
                    next_slot()
                while todo:
                    next_slot()
                if isinstance(v, int) and v == 0:
                    pe.wait_ge(s_qmore, (NCH - 1) * DT * BLOCKS * 16)

            each_unit(pe, body)
            attend(UNITS - 1, KT - 1, (UNITS - 1) % 2)

            def project(j):
                normalised(pe, (j + 1) * G - 1)
                for q in range(QT):
                    n = j * QT + q
                    if n >= 4:
                        pe.wait_ge(s_resid, n - 3)
                    for g in range(G):
                        mm = pe.matmul(ps[:, n % 4, 0:D], OT[:, (j * G + g) * CHUNK + q * P:(j * G + g) * CHUNK + (q + 1) * P],
                                       wo[:, g, :], start=(g == 0), stop=(g == G - 1))
                    mm.then_inc(s_proj, 1)

            def turn2(j):
                pe.wait_ge(s_n2, j + 1)
                if j:
                    pe.wait_ge(s_l2, j * DT)
                for dt in range(DT):
                    for q in range(QT):
                        mm = pe.transpose(ps[:, TURN_BANKS[dt], q * P:(q + 1) * P],
                                          xn2[:, j % 2, q, dt * P:(dt + 1) * P], ident[:])
                    mm.then_inc(s_turn2, 1)

            pe.wait_ge(s_wo, HPG * 16)
            pe.wait_ge(s_free, TOTAL_SLOTS)
            project(0)
            project(1)
            turn2(0)
            pe.wait_ge(s_rrow, UNITS * 16)
            pe.matmul(ps[:, LAST_BANK, :], select[:], rrow[:], start=True, stop=True).then_inc(s_slot, 1)
            project(2)
            turn2(1)
            project(3)
            turn2(2)

            def gate_up(i, k):
                n = i * 8 + k
                j, half = k % 4, k // 4 % 2
                cols = slice(j * CHUNK, (j + 1) * CHUNK)
                pe.wait_ge(s_l2, (j + 1) * DT)
                if j == 0:
                    pe.wait_ge(s_wlo, i * 2 + (k // 4 + 1))
                for f in range(FT):
                    idx = n * FT + f
                    for m, (filled, used) in enumerate(((s_gate, s_silu), (s_up, s_prod))):
                        if positive(idx - 1):
                            pe.wait_ge(used, idx - 1)
                        pairs = [(w, r, dt) for dt in range(DT) for w, r in
                                 ((w_hi, x2_hi), (w_hi, x2_lo), (w_lo, x2_hi))]
                        for a, (w, r, dt) in enumerate(pairs):
                            mm = pe.matmul(ps[:, 2 * (f % 2) + m, :],
                                           w[half][:, m, dt * F + f * P:dt * F + (f + 1) * P], r[:, dt, cols],
                                           start=(a == 0), stop=(a == len(pairs) - 1))
                        mm.then_inc(filled, 1)

            def down_rows(i, k):
                n = i * 8 + k
                half = k // 4 % 2
                pe.wait_ge(s_flo, n * FT + FT)
                for q in range(QT):
                    if positive(n):
                        pe.wait_ge(s_sum, n * QT + (q + 1 - QT))
                    pairs = [(a, w, f) for f in range(FT) for a, w in
                             ((f_hi, w_hi), (f_hi, w_lo), (f_lo, w_hi))]
                    for b, (a, w, f) in enumerate(pairs):
                        mm = pe.matmul(ps[:, 4 + q, 0:D], a[k % 2][:, f, q * P:(q + 1) * P],
                                       w[half][:, 2, f * D:(f + 1) * D], start=(b == 0), stop=(b == len(pairs) - 1))
                    mm.then_inc(s_down, 1)

            def logits(j):
                pe.wait_ge(s_rt2, 1)
                pe.wait_ge(s_free, TOTAL_SLOTS + 1)
                if j >= 2:
                    pe.wait_ge(s_lrows, j - 1)
                pe.wait_ge(s_l2, (j + 1) * DT)
                pairs = [(r, dt) for r in (x2_hi, x2_lo) for dt in range(DT)]
                for a, (r, dt) in enumerate(pairs):
                    mm = pe.matmul(ps[0:2 * E, LOGIT_BANKS[j % 2], :], rt2[:, dt, :],
                                   r[:, dt, j * CHUNK:(j + 1) * CHUNK],
                                   start=(a == 0), stop=(a == len(pairs) - 1))
                mm.then_inc(s_lraw, 1)

            def turn_logits(j):
                pe.wait_ge(s_l2, NCH * DT)
                pe.wait_ge(s_lrows, j + 1)
                for n in range(j * QT, (j + 1) * QT):
                    mm = pe.transpose(ps[:, ROUTE_BANK, n * 2 * E:(n + 1) * 2 * E],
                                      lrows[:, j, n % QT * P:(n % QT + 1) * P], ident[0:2 * E, 0:2 * E])
                return mm

            logits(0)
            logits(1)
            pe.wait_ge(s_resid, NTILES)
            gate_up(0, 0)
            turn2(NCH - 1)
            logits(2)

            def step(i, k):
                gate_up(i, k)
                if isinstance(i, int) and i == 0 and k == 1:
                    logits(3)
                    for j in range(NCH):
                        mm = turn_logits(j)
                    mm.then_inc(s_logit, 1)
                    pe.wait_ge(s_lread, 1)
                down_rows(i, k - 1)

            steps(pe, step)
            down_rows(E // 2 - 1, 7)


def kernel(x, ctx_512, L0_xattn_Wq, L0_xattn_Wkv, L0_xattn_Wo, L0_ffn_kernel_router_DE,
           L0_ffn_kernel_gating_EDF, L0_ffn_kernel_up_EDF, L0_ffn_kernel_down_EFD):
    import numpy as np
    import concourse.bacc as bacc
    from concourse.bass_utils import run_bass_kernel_spmd

    laid = {
        "x": np.asarray(x)[0],
        "ctxT": np.asarray(ctx_512)[0].T,
        "WqT": np.asarray(L0_xattn_Wq).T,
        "WkvT": np.asarray(L0_xattn_Wkv).T,
        "WoT": np.asarray(L0_xattn_Wo).T,
        "router": L0_ffn_kernel_router_DE,
        "gating": L0_ffn_kernel_gating_EDF,
        "up": L0_ffn_kernel_up_EDF,
        "down": L0_ffn_kernel_down_EFD,
    }
    nc = bacc.Bacc("TRN2", target_bir_lowering=False, num_devices=1)
    arrays, args = {}, {}
    for name, a in laid.items():
        a = np.ascontiguousarray(a)
        arrays[f"in_{name}"] = a
        args[name] = nc.dram_tensor(f"in_{name}", a.shape, mybir.dt.from_np(a.dtype), kind="ExternalInput").ap()
    shape = laid["x"].shape
    args["out"] = nc.dram_tensor("out_x", shape, F32, kind="ExternalOutput").ap()
    build(nc, **args)
    r = run_bass_kernel_spmd(nc, [arrays], core_ids=[0])
    return r.results[0]["out_x"].reshape((1,) + shape)
```

```python
from contextlib import ExitStack
import struct

import concourse.bass as bass
from concourse import mybir

F32, F32R, BF16 = mybir.dt.float32, mybir.dt.float32r, mybir.dt.bfloat16
ALU = mybir.AluOpType
ACT = mybir.ActivationFunctionType
AX = mybir.AxisListType

P = 128
LN_EPS = 1e-5
CHUNK = 512
QT = CHUNK // P
QUAD = 32
HPG = P // QUAD
DENROWS = 64
K_PARTS = (0, 1, 2, 0, 1, 0)
Q_PARTS = (0, 0, 0, 1, 1, 2)
BLOCKS = len(K_PARTS)
MAX_BANKS = (5, 6, 7)
JOB_BANKS = 5
O_BANK = 4
AHEAD = 24
TURN_LAG = 4
RECIP_SLOT = 13
RSPLIT_AT = 3
NORM_SLOT = 33
SPLIT_AT = 7
MERGE_AT = 9
DEVIATIONS_AT = 9


def positive(value):
    return not isinstance(value, int) or value > 0


def slots_of(v, last):
    steady = not isinstance(v, int)
    has_next = steady or v + 1 < last
    has_after = steady or v + 2 < last
    before = steady or v > 0
    rest = [("max", 1, i) for i in range(AHEAD, 64)] if has_next else [None] * NORM_SLOT
    more = [("max", 2, i) for i in range(AHEAD)] if has_after else []
    spread = [("spread", -1, 0)] if before else []
    turn = [("turn", 1, 0)] if has_next else []
    return rest[:NORM_SLOT] + spread + rest[NORM_SLOT:] + more[:TURN_LAG] + turn + more[TURN_LAG:]


def build(nc, x, ctxT, WqT, WkvT, WoT, router, gating, up, down, out):
    T, D = x.shape
    L, KEYS = ctxT.shape
    E, _, F = gating.shape
    DT = D // P
    FT = F // P
    NTILES = T // P
    NCH = T // CHUNK
    HEADS = 16
    HD = D // HEADS
    G = HEADS // HPG
    UNITS = NCH * G
    KT = -(-KEYS // P)
    LASTK = KEYS - (KT - 1) * P
    KPAD = KEYS + KEYS % 2
    ROWS = BLOCKS * HD
    CROWS = ROWS + 3
    SCALE = float(HD) ** -0.5
    STEP = KEYS // 4
    SLOTS = 66
    MT_HEADS = P // HD
    assert KT % 2 == 1 and L == P and HPG * (HD + 1) <= P and CROWS <= P and UNITS % 4 == 0
    PRO_SLOTS = 64 + 1 + AHEAD

    with ExitStack() as stack:
        def at(name, shape, dt, offset):
            return nc.alloc_sbuf_tensor_at(name, shape, dt, offset=offset)

        def sem(name):
            return stack.enter_context(nc.semaphore(name))

        K_BYTES = G * HPG * KPAD * 2
        Q_BYTES = UNITS * HPG * CHUNK * 2
        V_BYTES = G * KT * P * 4
        VC_BYTES = KT * P * 4
        P_BYTES = 2 * HPG * CHUNK * 4
        O_BYTES = UNITS * CHUNK * 4
        base = nc.sbuf_base + -nc.sbuf_base % 32
        end = nc.sbuf_usable_end
        k_at = base
        q_at = k_at + K_BYTES
        v_at = q_at + Q_BYTES
        vc_at = v_at + V_BYTES
        p_at = vc_at + VC_BYTES
        o_at = p_at + P_BYTES
        s_at = o_at + O_BYTES
        small = [s_at]

        def little(name, shape, dt):
            size = 4 if dt in (F32, F32R) else 2
            for n in shape[1:]:
                size *= n
            small[0] += -small[0] % 32
            t = at(name, shape, dt, small[0])
            small[0] += size
            assert small[0] <= end, name
            return t

        Kst = at("Kst", [P, G * HPG * KPAD], BF16, k_at)
        Qst = at("Qst", [P, UNITS * HPG * CHUNK], BF16, q_at)
        V = at("V", [P, G * KT * P], F32, v_at)
        Vcur = at("Vcur", [P, KT, P], F32, vc_at)
        probs = at("probs", [P, 2, HPG, CHUNK], F32, p_at)
        OT = at("OT", [P, UNITS * CHUNK], F32, o_at)
        xt = at("xt", [P, NCH, QT, D], F32, p_at)
        ctx_sb = at("ctx_sb", [P, KEYS], F32, vc_at)
        Kp = at("Kp", [P, DT, 3, KPAD], BF16, v_at)
        Qp = at("Qp", [P, DT, 3, T], BF16, o_at)
        wq = at("wq", [P, DT, D], F32, o_at + DT * 3 * T * 2)
        wkv = at("wkv", [P, 2 * D], F32, o_at + DT * 3 * T * 2 + DT * D * 4)
        xnT = [at("xnT0", [P, DT, CHUNK], F32, o_at + DT * 3 * T * 2 + DT * D * 4 + 2 * D * 4),
               at("xnT1", [P, DT, CHUNK], F32, v_at + DT * 3 * KPAD * 2 + 8)]
        WB = (2 * DT * F + FT * D) * 4
        acc = at("acc", [P, NTILES, D], F32, q_at)
        wraw = at("wraw", [P, 3, FT * D], F32, q_at + NTILES * D * 4)
        wo = at("wo", [P, G // 2, D], F32, q_at + NTILES * D * 4 + WB)
        wA = q_at + NTILES * D * 4 + WB + G // 2 * D * 4
        w_hi = [at("w_hi0", [P, 3, FT * D], F32R, wA), at("w_hi1", [P, 3, FT * D], F32R, k_at)]
        w_lo = [at("w_lo0", [P, 3, FT * D], F32R, wA + WB), at("w_lo1", [P, 3, FT * D], F32R, k_at + WB)]
        x2_hi = at("x2_hi", [P, DT, T], F32R, k_at + 2 * WB)
        x2_lo = at("x2_lo", [P, DT, T], F32R, v_at)
        xn2 = at("xn2", [P, 2, QT, D], F32, v_at + DT * T * 4)
        lrows = at("lrows", [2 * E, NCH, CHUNK], F32, v_at + DT * T * 4 + 2 * QT * D * 4)
        f_hi = [at("f_hi0", [P, FT, CHUNK], F32R, p_at), at("f_hi1", [P, FT, CHUNK], F32R, o_at)]
        f_lo = [at("f_lo0", [P, FT, CHUNK], F32R, p_at + FT * CHUNK * 4),
                at("f_lo1", [P, FT, CHUNK], F32R, o_at + FT * CHUNK * 4)]
        silu = at("silu", [P, 2, CHUNK], F32, o_at + 2 * FT * CHUNK * 4)
        prod = at("prod", [P, 2, CHUNK], F32, o_at + 2 * FT * CHUNK * 4 + 2 * CHUNK * 4)
        assert wA + 2 * WB <= v_at and DT * T * 4 + 2 * QT * D * 4 <= V_BYTES
        assert 2 * WB + DT * T * 4 <= K_BYTES
        assert DT * T * 4 + 2 * QT * D * 4 + NCH * CHUNK * 4 <= V_BYTES + VC_BYTES

        ident = little("ident", [P, P], F32)
        zeros = little("zeros", [P, 1, 1], F32)
        select = little("select", [HPG, 2, P], F32)
        select1 = little("select1", [HPG, 2, P], BF16)
        select3 = little("select3", [3 * HPG, 2, P], BF16)
        mx = little("mx", [P, 64], F32)
        cmax = little("cmax", [P, 16], F32)
        negc = little("negc", [16, P], F32)
        crest = little("crest", [16, P], F32)
        cpart = little("cpart", [16, 3, P], BF16)
        osb = little("osb", [P, CHUNK], F32)
        rest = [at("rest0", [P, CHUNK], F32, small[0] - CHUNK * 4), little("rest1", [P, CHUNK], F32)]
        rrow = at("rrow", [3 * HPG, CHUNK], BF16, small[0] - CHUNK * 4)
        den = little("den", [DENROWS, HPG * CHUNK // DENROWS], F32)
        rden = little("rden", [DENROWS, HPG * CHUNK // DENROWS], F32)
        rrest = little("rrest", [DENROWS, HPG * CHUNK // DENROWS], F32)
        rpart = little("rpart", [DENROWS, 3, HPG * CHUNK // DENROWS], BF16)
        stats = little("stats", [P, QT, 6], F32)
        mv = little("mv", [P, 2, QT, 2], F32)
        ve = little("ve", [P, 2, QT], F32)
        sd = little("sd", [P, 2, QT], F32)
        rs = little("rs", [P, QT], F32)
        nt = little("nt", [P, QT], F32)
        rt = little("rt", [P, DT, E], F32)
        rt2 = little("rt2", [P, DT, 2 * E], F32R)
        iota = little("iota", [P, NTILES, E], F32)
        rbase = o_at + 2 * FT * CHUNK * 4 + 4 * CHUNK * 4
        rn = [rbase]

        def routed(name, shape):
            n = 4
            for k in shape[1:]:
                n *= k
            t = at(name, shape, F32, rn[0])
            rn[0] += n + -n % 32
            assert rn[0] <= s_at
            return t

        W8 = [P, NTILES, E]
        W1 = [P, NTILES, 1]
        logit = routed("logit", W8)
        prob = routed("prob", W8)
        hot1 = routed("hot1", W8)
        hot2 = routed("hot2", W8)
        work = routed("work", W8)
        top1 = routed("top1", W1)
        top2 = routed("top2", W1)
        pick = routed("pick", W1)
        total = routed("total", W1)
        weight = routed("weight", [P, E * NTILES])

        ps = stack.enter_context(nc.psum_tensor("ps", [P, 8, CHUNK], F32))

        s_wkv, s_wq, s_ctx = sem("s_wkv"), sem("s_wq"), sem("s_ctx")
        s_x = [sem(f"s_x{j}") for j in range(NCH)]
        s_ident, s_pfill = sem("s_ident"), sem("s_pfill")
        s_stat, s_var, s_sd, s_xn = sem("s_stat"), sem("s_var"), sem("s_sd"), sem("s_xn")
        s_chain = sem("s_chain")
        s_job = sem("s_job")
        s_high, s_rest, s_mid, s_low = sem("s_high"), sem("s_rest"), sem("s_mid"), sem("s_low")
        s_xT, s_v, s_vzero, s_vone = sem("s_xT"), sem("s_v"), sem("s_vzero"), sem("s_vone")
        s_kout = [[sem(f"s_kout{mt}_{p}") for p in range(3)] for mt in range(DT)]
        s_qout = [[sem(f"s_qout{j}_{mt}") for mt in range(DT)] for j in range(NCH)]
        s_kin = [sem(f"s_kin{n}") for n in range(3)]
        s_qin = [sem(f"s_qin{mt}") for mt in range(DT)]
        s_qmore = sem("s_qmore")
        s_score, s_prob, s_av, s_vcur = sem("s_score"), sem("s_prob"), sem("s_av"), sem("s_vcur")
        s_slot, s_free = sem("s_slot"), sem("s_free")
        s_cmax, s_csplit, s_cpart, s_crow = sem("s_cmax"), sem("s_csplit"), sem("s_cpart"), sem("s_crow")
        s_osb, s_den, s_rden, s_rsplit = sem("s_osb"), sem("s_den"), sem("s_rden"), sem("s_rsplit")
        s_rpart, s_rrow, s_select1, s_select3 = sem("s_rpart"), sem("s_rrow"), sem("s_select1"), sem("s_select3")
        s_merge, s_acc, s_wo, s_rt = sem("s_merge"), sem("s_acc"), sem("s_wo"), sem("s_rt")
        s_proj, s_resid, s_n2, s_turn2 = sem("s_proj"), sem("s_resid"), sem("s_n2"), sem("s_turn2")
        s_h2, s_l2, s_rt2, s_route = sem("s_h2"), sem("s_l2"), sem("s_rt2"), sem("s_route")
        s_lraw, s_lrows, s_logit, s_lread = sem("s_lraw"), sem("s_lrows"), sem("s_logit"), sem("s_lread")
        s_shift, s_exp, s_iota = sem("s_shift"), sem("s_exp"), sem("s_iota")
        s_wraw, s_whi, s_wlo = sem("s_wraw"), sem("s_whi"), sem("s_wlo")
        s_gate, s_up, s_silu, s_prod = sem("s_gate"), sem("s_up"), sem("s_silu"), sem("s_prod")
        s_fhi, s_flo, s_down, s_sum, s_out = sem("s_fhi"), sem("s_flo"), sem("s_down"), sem("s_sum"), sem("s_out")

        kparts = nc.dram_tensor("kparts", [DT, 3, P, KEYS], BF16, kind="Internal").ap()
        qparts = nc.dram_tensor("qparts", [NCH, DT, BLOCKS, P, CHUNK], BF16, kind="Internal").ap()

        block = stack.enter_context(nc.Block())

        def prologue_slots():
            ahead = [("max", 1, i) for i in range(AHEAD)]
            return [("max", 0, i) for i in range(64)] + ahead[:TURN_LAG] + [("turn", 0, 0)] + ahead[TURN_LAG:]

        KC = [(k, min(CHUNK, KEYS - k)) for k in range(0, KEYS, CHUNK)]

        def turn_jobs(j):
            return [("T", j, dt) for dt in range(DT)]

        def query_jobs(j):
            return [(part, j, mt) for mt in range(DT) for part in "qQ"]

        def key_jobs(mt):
            return [("K", mt, kc) for kc in range(len(KC))]

        def norm(j):
            return [("N", j, 0), ("M", j, 0)]

        keys0 = key_jobs(0)
        early = (norm(0) + keys0[:1] + turn_jobs(0) + keys0[1:] + query_jobs(0)[:2] + norm(1) + query_jobs(0)[2:]
                 + key_jobs(1))
        late = []
        for j in range(1, NCH):
            late += turn_jobs(j)
            query = query_jobs(j)
            if j + 1 < NCH:
                query[1:1] = norm(j + 1)[:1]
                query[4:4] = norm(j + 1)[1:]
            late += query
        values_from = 46
        late_values = [("V", kt, 0) for kt in range(KT)]
        opening = list(early)
        for n, what in enumerate(prologue_slots()):
            opening.append(what)
            if n % 2:
                if late:
                    opening.append(late.pop(0))
                elif late_values and n >= values_from:
                    opening.append(late_values.pop(0))
        assert not late and not late_values
        jobs = [job for job in opening if job[0] in "KTQV"]
        number = {job: n for n, job in enumerate(jobs)}
        splits = [job for job in jobs if job[0] in "KQ"]
        nth_split = {job: n for n, job in enumerate(splits)}
        turns = [job for job in jobs if job[0] == "T"]
        nth_turn = {job: n for n, job in enumerate(turns)}

        def part(job, p):
            kind, a, b = job
            if kind == "K":
                k0, n = KC[b]
                return Kp[:, a, p, k0:k0 + n]
            return Qp[:, b, p, a * CHUNK:(a + 1) * CHUNK]

        def width(job):
            return KC[job[2]][1] if job[0] == "K" else CHUNK

        def emptied(eng, job):
            if job[0] in "KQ":
                eng.wait_ge(s_rest, nth_split[job] + 1)
            elif job[0] == "T":
                eng.wait_ge(s_xT, nth_turn[job] + 1)
            else:
                eng.wait_ge(s_v, job[1] + 1)

        def keys_of(t):
            return P if t < KT - 1 else LASTK

        def group_of(v):
            return v % G

        def slot_base(v):
            if isinstance(v, int) and v == 0:
                return PRO_SLOTS
            if isinstance(v, int) and v == UNITS - 1:
                return PRO_SLOTS - 1 + (UNITS - 1) * SLOTS - AHEAD
            return v * SLOTS + (PRO_SLOTS - 1)

        def bank_of(v, i):
            first = PRO_SLOTS if isinstance(v, int) and v == 0 else (
                slot_base(v) if isinstance(v, int) else PRO_SLOTS - 1)
            return MAX_BANKS[(first + i) % 3]

        beside = [b for b in MAX_BANKS if b != bank_of(UNITS - 1, 0)]

        def project_bank(n):
            return (beside if n < (NCH - 1) * QT else (O_BANK, LAST_BANK))[n % 2]

        def normalised(eng, u):
            if isinstance(u, int) and u >= UNITS - 2:
                eng.wait_ge(s_free, slot_base(UNITS - 1) + 1 + (u - (UNITS - 2)))
            else:
                eng.wait_ge(s_free, slot_base(u + 1) + (NORM_SLOT + 1))

        def turned(u):
            if isinstance(u, int) and u == 0:
                return 64 + TURN_LAG + 1
            lag = 0 if isinstance(u, int) and u == UNITS - 1 else TURN_LAG
            return (u - 1) * SLOTS + (PRO_SLOTS - 1 + 64 - AHEAD + 1 + lag + 1)

        def each_unit(eng, body):
            body(0, 0)
            with eng.Fori(0, (UNITS - 4) // 2) as pair:
                body(pair * 2 + 1, 1)
                body(pair * 2 + 2, 0)
            for v in range(UNITS - 3, UNITS):
                body(v, v % 2)

        def piece(i):
            c, qt, q = i // 16, i // 4 % 4, i % 4
            return c, qt, q * STEP, STEP if q < 3 else KEYS - 3 * STEP

        def steps(eng, step):
            with eng.Fori(0, E // 2 - 1) as i:
                for k in range(2, 10):
                    step(i, k)
            for k in range(2, 8):
                step(E // 2 - 1, k)

        TOTAL_SLOTS = slot_base(UNITS - 1) + 1
        LAST_BANK, TURN_BANKS = 7, (5, 6)
        LOGIT_BANKS, ROUTE_BANK = (7, O_BANK), 5

        @block.sync
        def _(sp):
            xv = x.rearrange("(j q p) d -> j p q d", j=NCH, p=P)
            sp.dma_start(xt[:, 0], xv[0]).then_inc(s_x[0], 16)
            sp.dma_start(wkv[:], WkvT).then_inc(s_wkv, 16)
            sp.dma_start(ctx_sb[:], ctxT).then_inc(s_ctx, 16)
            sp.dma_start(wq[:], WqT.rearrange("(t p) n -> p t n", p=P)).then_inc(s_wq, 16)
            for j in range(1, NCH):
                sp.dma_start(xt[:, j], xv[j]).then_inc(s_x[j], 16)
            sp.dma_start(rt[:], router.rearrange("(t p) e -> p t e", p=P)).then_inc(s_rt, 16)

            sp.wait_ge(s_select1, 1)
            for p in range(3):
                sp.dma_start(select3[p * HPG:(p + 1) * HPG], select1[:]).then_inc(s_select3, 16)

            Kv = Kst[:].rearrange("p (h k) -> p h k", k=KPAD)
            Qv = Qst[:].rearrange("p (j h i) -> p j h i", j=NCH, i=CHUNK)

            part_done = (s_high, s_mid, s_low)

            def keys_out(mt, p):
                sp.wait_ge(part_done[p], nth_split[("K", mt, len(KC) - 1)] + 1)
                sp.dma_start(kparts[mt, p], Kp[:, mt, p, 0:KEYS]).then_inc(s_kout[mt][p], 16)

            def keys_in(mt, p, h0, h1, done):
                b = (5, 3, 0)[p]
                for need in range(p + 1):
                    sp.wait_ge(s_kout[mt][need], 16)
                sp.dma_start(Kv[b * HD:(b + p + 1) * HD, mt * MT_HEADS + h0:mt * MT_HEADS + h1, 0:KEYS],
                             kparts[mt, 0:p + 1].rearrange("a (d h) k -> (a d) h k", d=HD)[:, h0:h1, :]).then_inc(done, 16)

            def queries_out(j, mt, p):
                b, n = Q_PARTS.index(p), Q_PARTS.count(p)
                sp.wait_ge(part_done[p], nth_split[("Q", j, mt)] + 1)
                sp.dma_start(qparts[j, mt, b:b + n].rearrange("b p i -> p b i"),
                             Qp[:, mt, p:p + 1, j * CHUNK:(j + 1) * CHUNK].to_broadcast([P, n, CHUNK])
                             ).then_inc(s_qout[j][mt], 16)

            def queries_in(j, mt, done):
                sp.wait_ge(s_qout[j][mt], 3 * 16)
                sp.dma_start(Qv[0:ROWS, j, mt * MT_HEADS:(mt + 1) * MT_HEADS, :],
                             qparts[j, mt].rearrange("b (d h) i -> (b d) h i", d=HD)).then_inc(done, 16)

            keys_out(0, 0)
            keys_out(0, 1)
            queries_out(0, 0, 0)
            keys_out(0, 2)
            keys_in(0, 0, 0, HPG, s_kin[0])
            queries_out(0, 0, 1)
            keys_in(0, 1, 0, HPG, s_kin[0])
            queries_out(0, 0, 2)
            keys_in(0, 2, 0, HPG, s_kin[0])
            queries_in(0, 0, s_qin[0])
            for p in range(3):
                keys_in(0, p, HPG, MT_HEADS, s_kin[1])
            for p in range(3):
                queries_out(0, 1, p)
            for p in range(3):
                keys_out(1, p)
            queries_in(0, 1, s_qin[1])
            for p in range(3):
                keys_in(1, p, 0, MT_HEADS, s_kin[2])
            for j in range(1, NCH):
                for mt in range(DT):
                    for p in range(3):
                        queries_out(j, mt, p)
                for mt in range(DT):
                    queries_in(j, mt, s_qmore)

            def send_crow(v):
                sp.wait_ge(s_cpart, v + 1)
                for p in range(3):
                    row = Qst[ROWS + p:ROWS + p + 1, bass.ds(v * (HPG * CHUNK), HPG * CHUNK)]
                    sp.dma_start(row.rearrange("o (t i) -> o t i", i=P), cpart[:, p, :]).then_inc(s_crow, 16)

            def spread_den(v, half):
                sp.wait_ge(s_osb, v + 1)
                sp.dma_start(den[:], osb[HD - half:P:QUAD, :].rearrange("c (e i) -> c e i", e=DENROWS // HPG)).then_inc(s_den, 16)
                sp.wait_ge(s_rpart, v + 1)
                if positive(v):
                    normalised(sp, v - 1)
                for p in range(3):
                    sp.dma_start(rrow[p * HPG:(p + 1) * HPG, :].rearrange("c (e i) -> c e i", e=DENROWS // HPG),
                                 rpart[:, p, :]).then_inc(s_rrow, 16)

            send_crow(0)

            def body(v, odd):
                if positive(v):
                    spread_den(v - 1, 1 - odd)
                if isinstance(v, int) and v == UNITS - 2:
                    sp.wait_ge(s_score, (UNITS - 2) * KT * HPG)
                    sp.dma_start(acc[:], x.rearrange("(n p) d -> p n d", p=P)).then_inc(s_acc, 16)
                    for c in range(HPG):
                        for half in range(2):
                            sp.dma_start(wo[c * QUAD + half * HD:c * QUAD + (half + 1) * HD, :, :],
                                         WoT.rearrange("(g h c d) n -> h c d g n", h=2, c=HPG,
                                                       d=HD)[half, c]).then_inc(s_wo, 16)
                    load_expert(0)
                if not isinstance(v, int) or v + 1 < UNITS:
                    send_crow(v + 1)

            def load_expert(e):
                if positive(e):
                    sp.wait_ge(s_wlo, e)
                sp.dma_start(wraw[:, 0].rearrange("p (t f) -> p t f", f=F),
                             gating.rearrange("e (t p) f -> p (e t) f", p=P)[:, bass.ds(e * DT, DT), :]).then_inc(s_wraw, 16)
                sp.dma_start(wraw[:, 1].rearrange("p (t f) -> p t f", f=F),
                             up.rearrange("e (t p) f -> p (e t) f", p=P)[:, bass.ds(e * DT, DT), :]).then_inc(s_wraw, 16)
                sp.dma_start(wraw[:, 2].rearrange("p (t n) -> p t n", n=D),
                             down.rearrange("e (t p) n -> p (e t) n", p=P)[:, bass.ds(e * FT, FT), :]).then_inc(s_wraw, 16)

            each_unit(sp, body)
            spread_den(UNITS - 1, 1)
            with sp.Fori(1, E) as e:
                load_expert(e)
            for j in range(NCH):
                sp.wait_ge(s_sum, (E - 1) * NTILES + (j + 1) * QT)
                sp.dma_start(out.rearrange("(j q p) d -> j p q d", j=NCH, p=P)[j],
                             acc[:, j * QT:(j + 1) * QT, :]).then_inc(s_out, 16)
            sp.wait_ge(s_out, 16 * NCH)

        @block.gpsimd
        def _(pool):
            pool.memset(ident[:], 0.0).then_inc(s_pfill, 1)
            pool.wait_ge(s_pfill, 1)
            pool.affine_select(out=ident[:], in_=ident[:], compare_op=ALU.not_equal, fill=1.0, base=0,
                               pattern=[[-1, P]], channel_multiplier=1).then_inc(s_ident, 1)
            pool.memset(zeros[:], 0.0).then_inc(s_iota, 1)
            pool.memset(select[:], 1.0).then_inc(s_pfill, 1)
            for half in range(2):
                pool.wait_ge(s_pfill, 2 + half)
                pool.affine_select(out=select[:, half, :], in_=select[:, half, :], compare_op=ALU.is_ge, fill=0.0,
                                   base=-half * HD, pattern=[[1, P]], channel_multiplier=-QUAD).then_inc(s_pfill, 1)
                pool.wait_ge(s_pfill, 3 + half)
                pool.affine_select(out=select[:, half, :], in_=select[:, half, :], compare_op=ALU.is_ge, fill=0.0,
                                   base=half * HD + HD - 1, pattern=[[-1, P]],
                                   channel_multiplier=QUAD).then_inc(s_ident, 1)
            def low(n):
                w = width(splits[n])
                pool.wait_ge(s_mid, n + 1)
                pool.tensor_tensor(part(splits[n], 2), rest[n % 2][:, 0:w], part(splits[n], 1),
                                   ALU.subtract).then_inc(s_low, 1)

            def clear_v(n, g0, g1):
                cols = V[:, g0 * KT * P:g1 * KT * P]
                pool.memset(cols, 0.0).then_inc(s_vzero, 1)
                pool.wait_ge(s_vzero, n)
                for half in range(2):
                    pool.memset(cols.rearrange("p (h n w) -> p h n w", h=2, w=QUAD)[:, half, :, HD - half:HD - half + 1],
                                1.0).then_inc(s_vone, 1)

            for n, job in enumerate(splits):
                low(n)
                if job == ("K", 1, len(KC) - 1):
                    two_ones = struct.unpack("<f", struct.pack("<I", 0x3F803F80))[0]
                    pool.wait_ge(s_low, n + 1)
                    pool.memset(Kst[ROWS:CROWS, :].bitcast(F32), two_ones).then_inc(s_ident, 1)
                    pool.wait_ge(s_ident, 4)
                if job == ("Q", 1, 1):
                    for mt in range(DT):
                        for p in range(3):
                            pool.wait_ge(s_kout[mt][p], 16)
                    clear_v(1, 0, 2)
            for k in range(E):
                pool.memset(iota[:, :, k:k + 1], float(k)).then_inc(s_iota, 1)
            pool.wait_ge(s_job, number[("Q", NCH - 1, DT - 1)] + 1)
            clear_v(2, 2, G)

            def copy_v(v, kt):
                n = keys_of(kt)
                if positive(v):
                    pool.wait_ge(s_av, v * KT + (kt + 1 - KT))
                pool.wait_ge(s_v, KT)
                pool.tensor_copy(Vcur[0:n, kt, :],
                                 V[0:n, bass.ds(group_of(v) * (KT * P) + kt * P, P)]).then_inc(s_vcur, 1)

            def split_c(v):
                pool.wait_ge(s_iota, 1)
                pool.wait_ge(s_free, turned(v))
                if positive(v):
                    pool.wait_ge(s_crow, v * 48)
                pool.tensor_tensor(cpart[:, 0, :], negc[:], zeros[0:16, 0].to_broadcast([16, P]), ALU.add).then_inc(s_csplit, 1)
                pool.wait_ge(s_csplit, v * 4 + 1)
                pool.tensor_tensor(crest[:], negc[:], cpart[:, 0, :], ALU.subtract).then_inc(s_csplit, 1)
                pool.wait_ge(s_csplit, v * 4 + 2)
                pool.tensor_tensor(cpart[:, 1, :], crest[:], zeros[0:16, 0].to_broadcast([16, P]), ALU.add).then_inc(s_csplit, 1)
                pool.wait_ge(s_csplit, v * 4 + 3)
                pool.tensor_tensor(negc[:], crest[:], cpart[:, 1, :], ALU.subtract).then_inc(s_csplit, 1)
                pool.wait_ge(s_csplit, v * 4 + 4)
                pool.tensor_tensor(cpart[:, 2, :], negc[:], zeros[0:16, 0].to_broadcast([16, P]), ALU.add).then_inc(s_cpart, 1)

            split_c(0)
            pool.wait_ge(s_v, KT)
            for kt in range(KT):
                copy_v(0, kt)

            def split_expert(e, half):
                pool.wait_ge(s_wraw, e * 48 + 48)
                if not isinstance(e, int):
                    pool.wait_ge(s_down, e * NTILES - NTILES)
                elif e == 1:
                    pool.wait_ge(s_score, UNITS * KT * HPG)
                pool.tensor_tensor(w_hi[half][:], wraw[:], zeros[:].to_broadcast([P, 3, FT * D]),
                                   ALU.add).then_inc(s_whi, 1)
                pool.wait_ge(s_whi, e + 1)
                pool.tensor_tensor(w_lo[half][:], wraw[:], w_hi[half][:].bitcast(F32),
                                   ALU.subtract).then_inc(s_wlo, 1)

            def split_r(v):
                none = zeros[0:DENROWS, 0].to_broadcast([DENROWS, HPG * CHUNK // DENROWS])
                pool.wait_ge(s_rden, v + 1)
                if positive(v):
                    pool.wait_ge(s_rrow, v * 48)
                pool.tensor_tensor(rpart[:, 0, :], rden[:], none, ALU.add).then_inc(s_rsplit, 1)
                pool.wait_ge(s_rsplit, v * 4 + 1)
                pool.tensor_tensor(rrest[:], rden[:], rpart[:, 0, :], ALU.subtract).then_inc(s_rsplit, 1)
                pool.wait_ge(s_rsplit, v * 4 + 2)
                pool.tensor_tensor(rpart[:, 1, :], rrest[:], none, ALU.add).then_inc(s_rsplit, 1)
                pool.wait_ge(s_rsplit, v * 4 + 3)
                pool.tensor_tensor(rden[:], rrest[:], rpart[:, 1, :], ALU.subtract).then_inc(s_rsplit, 1)
                pool.wait_ge(s_rsplit, v * 4 + 4)
                pool.tensor_tensor(rpart[:, 2, :], rden[:], none, ALU.add).then_inc(s_rpart, 1)

            def body(v, odd):
                if isinstance(v, int) and v == UNITS - 1:
                    split_r(v - 1)
                    return
                for kt in range(KT):
                    if kt == RSPLIT_AT and positive(v):
                        split_r(v - 1)
                    if kt == SPLIT_AT:
                        split_c(v + 1)
                    copy_v(v + 1, kt)
                    if kt == MERGE_AT and odd == 0 and positive(v):
                        normalised(pool, v - 1)
                        pair = OT[:, bass.ds(v * CHUNK - 2 * CHUNK, CHUNK)]
                        pool.tensor_tensor(pair, pair, OT[:, bass.ds(v * CHUNK - CHUNK, CHUNK)],
                                           ALU.add).then_inc(s_merge, 1)

            each_unit(pool, body)
            split_expert(0, 0)
            split_r(UNITS - 1)
            split_expert(1, 1)
            with pool.Fori(1, E // 2) as i:
                split_expert(i * 2, 0)
                split_expert(i * 2 + 1, 1)

        @block.scalar
        def _(act):
            def deviation(j):
                act.wait_ge(s_var, j + 1)
                act.activation(sd[:, j % 2, :], ve[:, j % 2, :], ACT.Sqrt).then_inc(s_sd, 1)

            def high(job):
                n = nth_split[job]
                act.wait_ge(s_job, number[job] + 1)
                act.copy(part(job, 0), ps[:, number[job] % JOB_BANKS, 0:width(job)]).then_inc(s_high, 1)

            def turned(job):
                _, j, dt = job
                act.wait_ge(s_job, number[job] + 1)
                if j >= 2:
                    act.wait_ge(s_job, number[("Q", j - 2, DT - 1)] + 1)
                act.copy(xnT[j % 2][:, dt, :], ps[:, number[job] % JOB_BANKS, :]).then_inc(s_xT, 1)

            def values(kt):
                n = keys_of(kt)
                job = number[("V", kt, 0)]
                act.wait_ge(s_job, job + 1)
                for half in range(2):
                    copied = act.copy(V[0:n, :].rearrange("p (g h k c w) -> p h k g c w", h=2, k=KT, c=HPG, w=QUAD)[
                                          :, half, kt, :, :, half * HD:(half + 1) * HD],
                                      ps[0:n, job % JOB_BANKS, 0:D].rearrange(
                                          "p (g h c d) -> p h g c d", h=2, c=HPG, d=HD)[:, half])
                copied.then_inc(s_v, 1)

            def middle(n):
                w = width(splits[n])
                act.wait_ge(s_rest, n + 1)
                act.copy(part(splits[n], 1), rest[n % 2][:, 0:w]).then_inc(s_mid, 1)

            act.wait_ge(s_ident, 3)
            act.copy(select1[:], select[:]).then_inc(s_select1, 1)
            at_once = (("K", 0, len(KC) - 1), ("Q", 0, 0), ("Q", 1, 1), splits[-1])
            for job in opening:
                if job[0] == "N":
                    deviation(job[1])
                elif job[0] == "T":
                    turned(job)
                elif job[0] == "V":
                    if job[1] == 0:
                        act.wait_ge(s_vone, 4)
                    values(job[1])
                elif job[0] in "KQ":
                    high(job)
                    if nth_split[job] and splits[nth_split[job] - 1] not in at_once:
                        middle(nth_split[job] - 1)
                    if job in at_once:
                        middle(nth_split[job])

            def exp(v, t, c, odd):
                n = keys_of(t)
                act.wait_ge(s_score, v * (KT * HPG) + (t * HPG + c + 1))
                if c == 0:
                    used = v * KT + (t - 1)
                    if positive(used):
                        act.wait_ge(s_av, used)
                act.activation(probs[0:n, (t + odd) % 2, c, :], ps[0:n, c, :], ACT.Exp, scale=SCALE).then_inc(s_prob, 1)

            def take_output(v):
                act.wait_ge(s_av, v * KT + KT)
                if positive(v):
                    normalised(act, v - 1)
                act.copy(osb[:], ps[:, O_BANK, :]).then_inc(s_osb, 1)

            def body(v, odd):
                for t in range(KT):
                    for c in range(HPG):
                        exp(v, t, c, odd)
                    if t == 0 and positive(v):
                        take_output(v - 1)
                    if isinstance(v, int) and v == UNITS - 1 and t == DEVIATIONS_AT:
                        deviation(NCH)
                        deviation(NCH + 1)

            each_unit(act, body)

            def high2(j):
                for dt in range(DT):
                    act.wait_ge(s_turn2, j * DT + dt + 1)
                    act.copy(x2_hi[:, dt, j * CHUNK:(j + 1) * CHUNK], ps[:, TURN_BANKS[dt], :]).then_inc(s_h2, 1)

            def hidden(i, k, tiles=range(FT)):
                n = i * 8 + k
                for f in tiles:
                    idx = n * FT + f
                    act.wait_ge(s_gate, idx + 1)
                    if positive(idx - 1):
                        act.wait_ge(s_prod, idx - 1)
                    act.activation(silu[:, f % 2, :], ps[:, 2 * (f % 2), :], ACT.Silu).then_inc(s_silu, 1)
                    act.wait_ge(s_prod, idx + 1)
                    if positive(n - 1):
                        act.wait_ge(s_down, n * QT - QT)
                    act.copy(f_hi[k % 2][:, f, :], prod[:, f % 2, :]).then_inc(s_fhi, 1)

            def take_logits(j):
                act.wait_ge(s_lraw, j + 1)
                act.copy(lrows[:, j, :], ps[0:2 * E, LOGIT_BANKS[j % 2], :]).then_inc(s_lrows, 1)

            high2(0)
            take_output(UNITS - 1)
            hidden(0, 0, range(0, FT // 2))
            high2(1)
            hidden(0, 0, range(FT // 2, FT))
            deviation(NCH + 2)
            deviation(NCH + 3)
            hidden(0, 1, range(0, 3))
            high2(2)
            hidden(0, 1, range(3, FT))
            take_logits(0)
            high2(3)
            for j in range(1, NCH):
                take_logits(j)
            act.wait_ge(s_shift, 1)
            act.activation(prob[:], work[:], ACT.Exp).then_inc(s_exp, 1)
            act.wait_ge(s_shift, 2)
            act.activation(total[:], pick[:], ACT.Exp).then_inc(s_exp, 1)
            steps(act, hidden)

        @block.vector
        def _(dve):
            links = [0]

            def link(instruction):
                links[0] += 1
                instruction.then_inc(s_chain, 1)
                dve.wait_ge(s_chain, links[0])

            def norm_stats(k, src):
                for q in range(QT):
                    dve.bn_stats(stats[:, q, :], src(q)).then_inc(s_stat, 1)
                dve.wait_ge(s_stat, k * 2 * QT + QT)
                for q in range(QT):
                    dve.bn_aggr(mv[:, k % 2, q, :], stats[:, q, :]).then_inc(s_stat, 1)
                dve.wait_ge(s_stat, (k + 1) * 2 * QT)
                dve.tensor_scalar(ve[:, k % 2, :], mv[:, k % 2, :, 1], LN_EPS, None, ALU.add).then_inc(s_var, 1)

            def norm_rows(k, src, dst):
                dve.wait_ge(s_sd, k + 1)
                link(dve.reciprocal(rs[:], sd[:, k % 2, :]))
                link(dve.tensor_tensor(nt[:], rs[:], rs[:], ALU.mult))
                link(dve.tensor_tensor(nt[:], nt[:], ve[:, k % 2, :], ALU.mult))
                link(dve.tensor_scalar(nt[:], nt[:], -0.5, 1.5, ALU.mult, ALU.add))
                link(dve.tensor_tensor(rs[:], rs[:], nt[:], ALU.mult))
                for q in range(QT):
                    last = dve.tensor_scalar(dst(q), src(q), mv[:, k % 2, q, 0:1], rs[:, q:q + 1],
                                             ALU.subtract, ALU.mult)
                    if q < QT - 1:
                        last.then_inc(s_chain, 1)
                        links[0] += 1
                return last

            def stats1(j):
                dve.wait_ge(s_x[j], 16)
                norm_stats(j, lambda q: xt[:, j, q, :])

            def norm1(j):
                norm_rows(j, lambda q: xt[:, j, q, :], lambda q: xt[:, j, q, :]).then_inc(s_xn, 1)

            def split(job):
                n, w = nth_split[job], width(job)
                dve.wait_ge(s_high, n + 1)
                if n >= 2:
                    dve.wait_ge(s_low, n - 1)
                dve.tensor_tensor(rest[n % 2][:, 0:w], ps[:, number[job] % JOB_BANKS, 0:w], part(job, 0),
                                  ALU.subtract).then_inc(s_rest, 1)

            def slot(v, count, bank, what, u):
                kind, _, i = what
                dve.wait_ge(s_slot, count)
                if kind == "max":
                    n = piece(i)[3]
                    dve.tensor_reduce(mx[:, i:i + 1], ps[:, bank, 0:n], AX.X, ALU.max).then_inc(s_free, 1)
                elif kind == "turn":
                    if positive(u):
                        dve.wait_ge(s_cpart, u)
                    dve.tensor_scalar(negc[:], ps[0:16, bank, 0:P], -1.0, None, ALU.mult).then_inc(s_free, 1)
                else:
                    dve.tensor_tensor(OT[:, bass.ds(u * CHUNK, CHUNK)], osb[:], ps[:, bank, :],
                                      ALU.mult).then_inc(s_free, 1)

            def row_max(u, count):
                dve.wait_ge(s_free, count)
                dve.tensor_reduce(cmax[:], mx[:].rearrange("p (a b) -> p a b", b=4), AX.X,
                                  ALU.max).then_inc(s_cmax, 1)
                dve.wait_ge(s_cmax, u + 1)

            def invert(u):
                dve.wait_ge(s_den, u * 16 + 16)
                if positive(u):
                    dve.wait_ge(s_rpart, u)
                dve.reciprocal(rden[:], den[:]).then_inc(s_rden, 1)

            n = 0
            waiting = []
            for step_no, what in enumerate(opening):
                while waiting and (waiting[0][0] <= step_no or what[0] in "NM" and n == 0):
                    split(waiting.pop(0)[1])
                if what[0] == "N":
                    stats1(what[1])
                elif what[0] == "M":
                    norm1(what[1])
                    if what[1] == NCH - 1:
                        dve.wait_ge(s_rt, 16)
                        link(dve.tensor_copy(rt2[:, :, 0:E], rt[:]))
                        dve.tensor_tensor(rt2[:, :, E:2 * E], rt[:], rt2[:, :, 0:E].bitcast(F32),
                                          ALU.subtract).then_inc(s_rt2, 1)
                elif what[0] in "KQ":
                    waiting.append((step_no + (3 if n else 0), what))
                elif what[0] in ("max", "turn"):
                    slot(0, n + 1, MAX_BANKS[n % 3], what, what[1])
                    n += 1
                    if what == ("max", 0, 63):
                        row_max(0, n)

            def residual(n):
                dve.wait_ge(s_proj, n + 1)
                dve.tensor_tensor(acc[:, n, :], ps[:, project_bank(n), 0:D], acc[:, n, :], ALU.add).then_inc(s_resid, 1)

            def stats2(j):
                dve.wait_ge(s_resid, (j + 1) * QT)
                norm_stats(NCH + j, lambda q: acc[:, j * QT + q, :])

            def norm2(j):
                if j:
                    dve.wait_ge(s_n2, j)
                if j >= 2:
                    dve.wait_ge(s_turn2, (j - 1) * DT)
                norm_rows(NCH + j, lambda q: acc[:, j * QT + q, :], lambda q: xn2[:, j % 2, q, :]).then_inc(s_n2, 1)

            def body(v, odd):
                first = slot_base(v)
                n = 0
                for i, what in enumerate(slots_of(v, UNITS)):
                    if i == RECIP_SLOT and positive(v):
                        if isinstance(v, int) and v == UNITS - 1:
                            dve.wait_ge(s_acc, 16)
                            for tile in range(3):
                                residual(tile)
                        invert(v - 1)
                    if what is None:
                        continue
                    if isinstance(v, int) and v == UNITS - 1:
                        residual(3)
                        stats2(0)
                        residual(4)
                    slot(v, first + (n + 1), bank_of(v, n), what, v + what[1])
                    n += 1
                    if what == ("max", 1, 63):
                        row_max(v + 1, first + n)

            each_unit(dve, body)

            for n in range(5, 2 * QT):
                residual(n)
            stats2(1)
            residual(2 * QT)
            dve.wait_ge(s_vcur, UNITS * KT)
            norm2(0)
            norm2(1)
            for n in range(2 * QT + 1, 3 * QT):
                residual(n)

            def low2(j):
                for dt in range(DT):
                    cols = slice(j * CHUNK, (j + 1) * CHUNK)
                    dve.wait_ge(s_h2, j * DT + dt + 1)
                    dve.tensor_tensor(x2_lo[:, dt, cols], ps[:, TURN_BANKS[dt], :],
                                      x2_hi[:, dt, cols].bitcast(F32), ALU.subtract).then_inc(s_l2, 1)

            def product(i, k, tiles=range(FT)):
                n = i * 8 + k
                for f in tiles:
                    idx = n * FT + f
                    dve.wait_ge(s_up, idx + 1)
                    dve.wait_ge(s_silu, idx + 1)
                    if positive(idx - 1):
                        dve.wait_ge(s_fhi, idx - 1)
                    dve.tensor_tensor(prod[:, f % 2, :], silu[:, f % 2, :], ps[:, 2 * (f % 2) + 1, :],
                                      ALU.mult).then_inc(s_prod, 1)
                    dve.wait_ge(s_fhi, idx + 1)
                    dve.tensor_tensor(f_lo[k % 2][:, f, :], prod[:, f % 2, :], f_hi[k % 2][:, f, :].bitcast(F32),
                                      ALU.subtract).then_inc(s_flo, 1)

            def add_up(i, k):
                n = i * 8 + k
                e = i * 2 + k // 4
                for q in range(QT):
                    tile = k % 4 * QT + q
                    dve.wait_ge(s_down, n * QT + (q + 1))
                    dve.scalar_tensor_tensor(acc[:, tile, :], ps[:, 4 + q, 0:D],
                                             weight[:, bass.ds(e * NTILES + tile, 1)], acc[:, tile, :],
                                             op0=ALU.mult, op1=ALU.add).then_inc(s_sum, 1)

            def step(i, k):
                product(i, k)
                add_up(i, k - 1)

            def route():
                wide = lambda a: a[:].to_broadcast(W8)
                lv = ps[:, ROUTE_BANK, 0:NTILES * 2 * E].rearrange("p (n w) -> p n w", w=2 * E)
                dve.wait_ge(s_logit, 1)
                link(dve.tensor_copy(logit[:], lv[:, :, 0:E]))
                dve.tensor_tensor(logit[:], logit[:], lv[:, :, E:2 * E], ALU.add).then_inc(s_lread, 1)
                dve.wait_ge(s_lread, 1)
                link(dve.tensor_reduce(top1[:], logit[:], AX.X, ALU.max))
                dve.tensor_tensor(work[:], logit[:], wide(top1), ALU.subtract).then_inc(s_shift, 1)
                dve.wait_ge(s_exp, 1)
                link(dve.tensor_reduce(total[:], prob[:], AX.X, ALU.add))
                link(dve.reciprocal(pick[:], total[:]))
                link(dve.tensor_tensor(prob[:], prob[:], wide(pick), ALU.mult))

                def first_largest(top, hot):
                    link(dve.tensor_reduce(top[:], prob[:], AX.X, ALU.max))
                    link(dve.tensor_tensor(hot[:], prob[:], wide(top), ALU.is_equal))
                    link(dve.scalar_tensor_tensor(work[:], hot[:], -float(E), iota[:], op0=ALU.mult, op1=ALU.add))
                    link(dve.tensor_reduce(pick[:], work[:], AX.X, ALU.min))
                    link(dve.tensor_tensor(hot[:], work[:], wide(pick), ALU.is_equal))

                dve.wait_ge(s_iota, 1 + E)
                first_largest(top1, hot1)
                link(dve.scalar_tensor_tensor(prob[:], hot1[:], -2.0, prob[:], op0=ALU.mult, op1=ALU.add))
                first_largest(top2, hot2)
                dve.tensor_tensor(pick[:], top2[:], top1[:], ALU.subtract).then_inc(s_shift, 1)
                dve.wait_ge(s_exp, 2)
                link(dve.tensor_scalar(top1[:], total[:], 1.0, None, ALU.add))
                link(dve.reciprocal(top1[:], top1[:]))
                link(dve.tensor_tensor(top2[:], total[:], top1[:], ALU.mult))
                link(dve.tensor_tensor(hot1[:], hot1[:], wide(top1), ALU.mult))
                link(dve.tensor_tensor(hot2[:], hot2[:], wide(top2), ALU.mult))
                dve.tensor_tensor(weight[:].rearrange("p (e n) -> p n e", n=NTILES), hot1[:], hot2[:],
                                  ALU.add).then_inc(s_route, 1)
                dve.wait_ge(s_route, 1)

            low2(0)
            stats2(2)
            invert(UNITS - 1)
            product(0, 0, range(0, FT // 2))
            low2(1)
            product(0, 0, range(FT // 2, FT // 2 + 1))
            last = OT[:, (UNITS - 1) * CHUNK:UNITS * CHUNK]
            pair = OT[:, (UNITS - 2) * CHUNK:(UNITS - 1) * CHUNK]
            dve.wait_ge(s_slot, TOTAL_SLOTS + 1)
            dve.tensor_tensor(last, osb[:], ps[:, LAST_BANK, :], ALU.mult).then_inc(s_free, 1)
            dve.wait_ge(s_free, TOTAL_SLOTS + 1)
            dve.tensor_tensor(pair, pair, last, ALU.add).then_inc(s_merge, 1)
            product(0, 0, range(FT // 2 + 1, FT))
            for n in range((NCH - 1) * QT, NTILES):
                residual(n)
            stats2(3)
            norm2(2)
            product(0, 1, range(0, 1))
            norm2(3)
            product(0, 1, range(1, 3))
            low2(2)
            product(0, 1, range(3, FT))
            low2(3)
            route()
            add_up(0, 0)
            steps(dve, step)
            add_up(E // 2 - 1, 7)

        @block.tensor
        def _(pe):
            pe.wait_ge(s_wkv, 16)
            pe.wait_ge(s_ctx, 16)
            def fill(job):
                kind, a, b = job
                n = number[(kind.upper(), a, b)]
                bank = ps[:, n % JOB_BANKS, :]
                if n >= JOB_BANKS and kind != "Q":
                    emptied(pe, jobs[n - JOB_BANKS])
                if kind == "K":
                    k0, w = KC[b]
                    pe.matmul(bank[:, 0:w], wkv[:, a * P:(a + 1) * P], ctx_sb[:, k0:k0 + w],
                              start=True, stop=True).then_inc(s_job, 1)
                elif kind == "T":
                    pe.wait_ge(s_ident, 1)
                    pe.wait_ge(s_xn, a + 1)
                    for q in range(QT):
                        mm = pe.transpose(bank[:, q * P:(q + 1) * P], xt[:, a, q, b * P:(b + 1) * P], ident[:])
                    mm.then_inc(s_job, 1)
                elif kind == "q":
                    pe.wait_ge(s_wq, 16)
                    pe.wait_ge(s_xT, (a + 1) * DT)
                    for dt in range(DT - 1):
                        pe.matmul(bank, wq[:, dt, b * P:(b + 1) * P], xnT[a % 2][:, dt, :], start=(dt == 0), stop=False)
                elif kind == "Q":
                    pe.matmul(bank, wq[:, DT - 1, b * P:(b + 1) * P], xnT[a % 2][:, DT - 1, :],
                              start=False, stop=True).then_inc(s_job, 1)
                else:
                    w = keys_of(a)
                    pe.matmul(bank[0:w, 0:D], ctx_sb[:, a * P:a * P + w], wkv[:, D:2 * D],
                              start=True, stop=True).then_inc(s_job, 1)

            def slot(v, before, bank, what, u, half=None):
                kind, _, i = what
                if positive(before - 2):
                    pe.wait_ge(s_free, before - 2)
                if kind == "max":
                    c, qt, k0, n = piece(i)
                    g = group_of(u)
                    pe.matmul(ps[:, bank, 0:n],
                              Qst[0:ROWS, bass.ds(u * (HPG * CHUNK) + (c * CHUNK + qt * P), P)],
                              Kst[0:ROWS, bass.ds(g * (HPG * KPAD) + (c * KPAD + k0), n)],
                              start=True, stop=True).then_inc(s_slot, 1)
                elif kind == "turn":
                    pe.wait_ge(s_cmax, u + 1)
                    pe.transpose(ps[0:16, bank, 0:P], cmax[:], ident[:]).then_inc(s_slot, 1)
                else:
                    pe.wait_ge(s_rrow, u * 48 + 48)
                    pe.matmul(ps[:, bank, :], select3[:, half, :], rrow[:], start=True, stop=True).then_inc(s_slot, 1)

            def stacked(g):
                pe.wait_ge(s_kin[min(g, 2)], 3 * 16)
                pe.wait_ge(s_qin[g // 2], 16)

            n = 0
            for what in opening:
                if what[0] in ("max", "turn"):
                    if n == 0:
                        stacked(0)
                    if what == ("max", 1, 0):
                        stacked(1)
                    slot(0, n, MAX_BANKS[n % 3], what, what[1])
                    n += 1
                elif what[0] not in "NM":
                    fill(what)
            for job in jobs[-JOB_BANKS:]:
                emptied(pe, job)

            def score(v, t, c):
                n = keys_of(t)
                g = group_of(v)
                done = v * (KT * HPG) + (t * HPG + c + 1 - HPG)
                if positive(done):
                    pe.wait_ge(s_prob, done)
                pe.matmul(ps[0:n, c, :],
                          Kst[0:CROWS, bass.ds(g * (HPG * KPAD) + (c * KPAD + t * P), n)],
                          Qst[0:CROWS, bass.ds(v * (HPG * CHUNK) + c * CHUNK, CHUNK)],
                          start=True, stop=True).then_inc(s_score, 1)

            def attend(v, t, odd):
                n = keys_of(t)
                pe.wait_ge(s_prob, v * (KT * HPG) + (t * HPG + HPG))
                pe.wait_ge(s_vcur, v * KT + (t + 1))
                if t == 0 and positive(v):
                    pe.wait_ge(s_osb, v)
                for c in range(HPG):
                    mm = pe.matmul(ps[c * QUAD:(c + 1) * QUAD, O_BANK, :], Vcur[0:n, t, c * QUAD:(c + 1) * QUAD],
                                   probs[0:n, (t + odd) % 2, c, :], start=(t == 0), stop=(t == KT - 1))
                mm.then_inc(s_av, 1)

            def project(n):
                if n == 0:
                    pe.wait_ge(s_wo, HPG * 2 * 16)
                    pe.wait_ge(s_free, slot_base(UNITS - 1))
                pe.wait_ge(s_merge, (n // QT + 1) * G // 2)
                if n == (NCH - 1) * QT:
                    pe.wait_ge(s_osb, UNITS)
                    pe.wait_ge(s_free, TOTAL_SLOTS + 1)
                elif n >= 2 and n != (NCH - 1) * QT + 1:
                    pe.wait_ge(s_resid, n - 1)
                for p in range(G // 2):
                    at_pair = (n // QT * G + 2 * p) * CHUNK + n % QT * P
                    mm = pe.matmul(ps[:, project_bank(n), 0:D], OT[:, at_pair:at_pair + P],
                                   wo[:, p, :], start=(p == 0), stop=(p == G // 2 - 1))
                mm.then_inc(s_proj, 1)

            def turn2(j):
                pe.wait_ge(s_n2, j + 1)
                if j:
                    pe.wait_ge(s_l2, j * DT)
                for dt in range(DT):
                    for q in range(QT):
                        mm = pe.transpose(ps[:, TURN_BANKS[dt], q * P:(q + 1) * P],
                                          xn2[:, j % 2, q, dt * P:(dt + 1) * P], ident[:])
                    mm.then_inc(s_turn2, 1)

            def body(v, odd):
                first = slot_base(v)
                todo = list(enumerate(slots_of(v, UNITS)))
                n = [0]

                def next_slot():
                    if not todo:
                        return
                    _, what = todo.pop(0)
                    if what is None:
                        return
                    if isinstance(v, int) and v == 0 and what == ("max", 2, 0):
                        stacked(2)
                    slot(v, first + n[0], bank_of(v, n[0]), what, v + what[1], 1 - odd)
                    n[0] += 1

                if isinstance(v, int) and v == 0:
                    pe.wait_ge(s_select3, 48)
                    pe.wait_ge(s_ident, 4)
                pe.wait_ge(s_crow, v * 48 + 48)
                for t in range(KT):
                    for c in range(HPG):
                        score(v, t, c)
                        next_slot()
                    if t:
                        attend(v, t - 1, odd)
                    elif positive(v):
                        attend(v - 1, KT - 1, 1 - odd)
                    next_slot()
                    if isinstance(v, int) and v == UNITS - 1 and t:
                        project(t - 1)
                while todo:
                    next_slot()
                if isinstance(v, int) and v == 0:
                    pe.wait_ge(s_qmore, (NCH - 1) * DT * 16)

            each_unit(pe, body)
            pe.wait_ge(s_resid, 3 * QT)
            turn2(0)
            attend(UNITS - 1, KT - 1, (UNITS - 1) % 2)

            def gate_up(i, k, tiles=range(FT)):
                n = i * 8 + k
                j, half = k % 4, k // 4 % 2
                cols = slice(j * CHUNK, (j + 1) * CHUNK)
                pe.wait_ge(s_l2, (j + 1) * DT)
                if j == 0:
                    pe.wait_ge(s_wlo, i * 2 + (k // 4 + 1))
                for f in tiles:
                    idx = n * FT + f
                    for m, (filled, used) in enumerate(((s_gate, s_silu), (s_up, s_prod))):
                        if positive(idx - 1):
                            pe.wait_ge(used, idx - 1)
                        pairs = [(w, r, dt) for dt in range(DT) for w, r in
                                 ((w_hi, x2_hi), (w_hi, x2_lo), (w_lo, x2_hi))]
                        for a, (w, r, dt) in enumerate(pairs):
                            mm = pe.matmul(ps[:, 2 * (f % 2) + m, :],
                                           w[half][:, m, dt * F + f * P:dt * F + (f + 1) * P], r[:, dt, cols],
                                           start=(a == 0), stop=(a == len(pairs) - 1))
                        mm.then_inc(filled, 1)

            def down_rows(i, k):
                n = i * 8 + k
                half = k // 4 % 2
                pe.wait_ge(s_flo, n * FT + FT)
                for q in range(QT):
                    if positive(n):
                        pe.wait_ge(s_sum, n * QT + (q + 1 - QT))
                    pairs = [(a, w, f) for f in range(FT) for a, w in
                             ((f_hi, w_hi), (f_hi, w_lo), (f_lo, w_hi))]
                    for b, (a, w, f) in enumerate(pairs):
                        mm = pe.matmul(ps[:, 4 + q, 0:D], a[k % 2][:, f, q * P:(q + 1) * P],
                                       w[half][:, 2, f * D:(f + 1) * D], start=(b == 0), stop=(b == len(pairs) - 1))
                    mm.then_inc(s_down, 1)

            def logits(j):
                pe.wait_ge(s_rt2, 1)
                if j < 2:
                    pe.wait_ge(s_resid, NTILES)
                else:
                    pe.wait_ge(s_lrows, j - 1)
                pe.wait_ge(s_l2, (j + 1) * DT)
                pairs = [(r, dt) for r in (x2_hi, x2_lo) for dt in range(DT)]
                for a, (r, dt) in enumerate(pairs):
                    mm = pe.matmul(ps[0:2 * E, LOGIT_BANKS[j % 2], :], rt2[:, dt, :],
                                   r[:, dt, j * CHUNK:(j + 1) * CHUNK],
                                   start=(a == 0), stop=(a == len(pairs) - 1))
                mm.then_inc(s_lraw, 1)

            def turn_logits(j):
                pe.wait_ge(s_l2, NCH * DT)
                pe.wait_ge(s_lrows, j + 1)
                for n in range(j * QT, (j + 1) * QT):
                    mm = pe.transpose(ps[:, ROUTE_BANK, n * 2 * E:(n + 1) * 2 * E],
                                      lrows[:, j, n % QT * P:(n % QT + 1) * P], ident[0:2 * E, 0:2 * E])
                return mm

            gate_up(0, 0, range(0, FT // 2))
            turn2(1)
            gate_up(0, 0, range(FT // 2, FT // 2 + 1))
            pe.wait_ge(s_rrow, UNITS * 48)
            pe.matmul(ps[:, LAST_BANK, :], select3[:, 1, :], rrow[:], start=True, stop=True).then_inc(s_slot, 1)
            gate_up(0, 0, range(FT // 2 + 1, FT))
            for n in range((NCH - 1) * QT, NTILES):
                project(n)
            gate_up(0, 1, range(0, 3))
            turn2(2)
            gate_up(0, 1, range(3, FT))
            logits(0)
            turn2(3)
            for j in range(1, NCH):
                logits(j)
            for j in range(NCH):
                mm = turn_logits(j)
            mm.then_inc(s_logit, 1)
            pe.wait_ge(s_lread, 1)
            down_rows(0, 0)

            def step(i, k):
                gate_up(i, k)
                down_rows(i, k - 1)

            steps(pe, step)
            down_rows(E // 2 - 1, 7)


def kernel(x, ctx_512, L0_xattn_Wq, L0_xattn_Wkv, L0_xattn_Wo, L0_ffn_kernel_router_DE,
           L0_ffn_kernel_gating_EDF, L0_ffn_kernel_up_EDF, L0_ffn_kernel_down_EFD):
    import numpy as np
    import concourse.bacc as bacc
    from concourse.bass_utils import run_bass_kernel_spmd

    def dimension_major(w, n):
        hd = n // 16
        first = w[:, :n].reshape(w.shape[0], n // P, P // hd, hd).transpose(0, 1, 3, 2).reshape(w.shape[0], n)
        return np.concatenate([first, w[:, n:]], axis=1)

    width = np.asarray(x).shape[2]
    laid = {
        "x": np.asarray(x)[0],
        "ctxT": np.asarray(ctx_512)[0].T,
        "WqT": dimension_major(np.asarray(L0_xattn_Wq).T, width),
        "WkvT": dimension_major(np.asarray(L0_xattn_Wkv).T, width),
        "WoT": np.asarray(L0_xattn_Wo).T,
        "router": L0_ffn_kernel_router_DE,
        "gating": L0_ffn_kernel_gating_EDF,
        "up": L0_ffn_kernel_up_EDF,
        "down": L0_ffn_kernel_down_EFD,
    }
    nc = bacc.Bacc("TRN2", target_bir_lowering=False, num_devices=1)
    arrays, args = {}, {}
    for name, a in laid.items():
        a = np.ascontiguousarray(a)
        arrays[f"in_{name}"] = a
        args[name] = nc.dram_tensor(f"in_{name}", a.shape, mybir.dt.from_np(a.dtype), kind="ExternalInput").ap()
    shape = laid["x"].shape
    args["out"] = nc.dram_tensor("out_x", shape, F32, kind="ExternalOutput").ap()
    build(nc, **args)
    r = run_bass_kernel_spmd(nc, [arrays], core_ids=[0])
    return r.results[0]["out_x"].reshape((1,) + shape)
```
